# Optimizing a Trainium2 kernel written in Bass

```python
import numpy as np
import jax
import jax.numpy as jnp

def _softmax(x, axis=-1):
    return jax.nn.softmax(x, axis=axis)

def _gelu(x):
    return jax.nn.gelu(x, approximate=True)

def _silu(x):
    return jax.nn.silu(x)

def _sigmoid(x):
    return jax.nn.sigmoid(x)

def _layernorm(x, axis=-1, eps=1e-05):
    m = jnp.mean(x, axis=axis, keepdims=True)
    v = jnp.var(x, axis=axis, keepdims=True)
    return (x - m) / jnp.sqrt(v + eps)

def _scatter_add(tgt, idx, src, axis=0):
    return tgt.at[idx].add(src)

def _segment_sum(src, seg, n):
    return jax.ops.segment_sum(src, seg, n)
kernel_name = 'mk_cond_resid_d2_seqx_r2_dc7161'

def setup_inputs(seed: int=0):
    np.random.seed(seed)
    _w = jnp.asarray

    def _rec_inputs():
        import jax
        import jax.numpy as jnp
        _rk = jax.random.key(seed)
        x = 2.818e-05 + 1 * jax.random.normal(jax.random.fold_in(_rk, 1), (4, 1024, 512), jnp.float32)
        _lenS = 1024 - jax.random.randint(jax.random.fold_in(_rk, 7), (4,), 0, max(1, 1024 // 4) + 1, jnp.int32)
        _lenS2 = 1024 - jax.random.randint(jax.random.fold_in(_rk, 8), (4,), 0, max(1, 1024 // 4) + 1, jnp.int32)
        cond_1024 = 0.00185052 + 1.01138 * jax.random.normal(jax.random.fold_in(_rk, 11), (4, 512), jnp.float32)
        itok_BxS_2_50255 = jax.random.randint(jax.random.fold_in(_rk, 12), (4, 1024), 2, 25128, jnp.int32)
        return (x, cond_1024, itok_BxS_2_50255)
    x, cond_1024, itok_BxS_2_50255 = _rec_inputs()

    def _L0_cond_setup():
        import jax, jax.numpy as jnp
        import numpy as np
        D = 512
        key = jax.random.key(seed)
        ks = jax.random.split(key, 12)
        sc_in = 1.0 / np.sqrt(D)
        sc_in2 = 1.0 / np.sqrt(2 * D)
        inp = {'X1': jax.random.normal(ks[0], (8, D), dtype=jnp.float32), 'X2': jax.random.normal(ks[1], (8, 1024, D), dtype=jnp.float32), 'Wq1': jax.random.normal(ks[2], (D, D), dtype=jnp.float32) * sc_in, 'bq1': jax.random.normal(ks[3], (D,), dtype=jnp.float32) * 0.01, 'Wq2': jax.random.normal(ks[4], (D, D), dtype=jnp.float32) * sc_in, 'bq2': jax.random.normal(ks[5], (D,), dtype=jnp.float32) * 0.01, 'Wk1': jax.random.normal(ks[6], (D, D), dtype=jnp.float32) * sc_in, 'bk1': jax.random.normal(ks[7], (D,), dtype=jnp.float32) * 0.01, 'Wk2': jax.random.normal(ks[8], (D, D), dtype=jnp.float32) * sc_in, 'bk2': jax.random.normal(ks[9], (D,), dtype=jnp.float32) * 0.01, 'Wv': jax.random.normal(ks[10], (2 * D, D), dtype=jnp.float32) * sc_in2, 'bv': jax.random.normal(ks[11], (D,), dtype=jnp.float32) * 0.01, 'alpha': jnp.float32(0.5)}
        return inp
    _L0_cond_all = _L0_cond_setup()
    _L0_cond_in = {k: v for k, v in _L0_cond_all.items() if k in ('Wq1', 'bq1', 'Wq2', 'bq2', 'Wk1', 'bk1', 'Wk2', 'bk2', 'Wv', 'bv', 'alpha')}
    del _L0_cond_all

    def _L1_cond_setup():
        import jax, jax.numpy as jnp
        import numpy as np
        HASH_PRIME = 5099
        MIN_CAPACITY = 4
        key = jax.random.key(seed)
        ks = jax.random.split(key, 8)
        B, T, D, F, E = (8, 1024, 512, 1024, 16)
        return {'x': jax.random.normal(ks[0], (B, T, D), dtype=jnp.float32), 'token_ids': jax.random.randint(ks[1], (B, T), 0, 50257, dtype=jnp.int32), 'shift_state': jax.random.normal(ks[2], (B, D), dtype=jnp.float32), 'time_maa_k': jax.random.uniform(ks[3], (D,), dtype=jnp.float32), 'time_maa_r': jax.random.uniform(ks[4], (D,), dtype=jnp.float32), 'w_recept': jax.random.normal(ks[5], (D, D), dtype=jnp.float32) * 0.02, 'w_key': jax.random.normal(ks[6], (E, D, F), dtype=jnp.float32) * 0.02, 'w_value': jax.random.normal(ks[7], (E, F, D), dtype=jnp.float32) * 0.02}
    _L1_cond_all = _L1_cond_setup()
    _L1_cond_in = {k: v for k, v in _L1_cond_all.items() if k in ('time_maa_k', 'time_maa_r', 'w_recept', 'w_key', 'w_value')}
    del _L1_cond_all
    return {'x': x, 'cond_1024': cond_1024, 'itok_BxS_2_50255': itok_BxS_2_50255, 'L0_cond_Wq1': _L0_cond_in['Wq1'], 'L0_cond_bq1': _L0_cond_in['bq1'], 'L0_cond_Wq2': _L0_cond_in['Wq2'], 'L0_cond_bq2': _L0_cond_in['bq2'], 'L0_cond_Wk1': _L0_cond_in['Wk1'], 'L0_cond_bk1': _L0_cond_in['bk1'], 'L0_cond_Wk2': _L0_cond_in['Wk2'], 'L0_cond_bk2': _L0_cond_in['bk2'], 'L0_cond_Wv': _L0_cond_in['Wv'], 'L0_cond_bv': _L0_cond_in['bv'], 'L0_cond_alpha': _L0_cond_in['alpha'], 'L1_cond_time_maa_k': _L1_cond_in['time_maa_k'], 'L1_cond_time_maa_r': _L1_cond_in['time_maa_r'], 'L1_cond_w_recept': _L1_cond_in['w_recept'], 'L1_cond_w_key': _L1_cond_in['w_key'], 'L1_cond_w_value': _L1_cond_in['w_value']}

def reference(x, cond_1024, itok_BxS_2_50255, L0_cond_Wq1, L0_cond_bq1, L0_cond_Wq2, L0_cond_bq2, L0_cond_Wk1, L0_cond_bk1, L0_cond_Wk2, L0_cond_bk2, L0_cond_Wv, L0_cond_bv, L0_cond_alpha, L1_cond_time_maa_k, L1_cond_time_maa_r, L1_cond_w_recept, L1_cond_w_key, L1_cond_w_value):
    import jax
    import jax.numpy as jnp

    def _L0_cond_ref(X1, X2, Wq1, bq1, Wq2, bq2, Wk1, bk1, Wk2, bk2, Wv, bv, alpha):
        import jax, jax.numpy as jnp
        import numpy as np
        D = 512
        B, S, Dm = X2.shape
        X1e = jnp.broadcast_to(X1[:, None, :], (B, S, Dm))
        X = jnp.concatenate([X1e, X2], axis=-1)
        Q1 = X1e @ Wq1 + bq1
        K1 = X1e @ Wk1 + bk1
        Q2 = X2 @ Wq2 + bq2
        K2 = X2 @ Wk2 + bk2
        V = X @ Wv + bv
        s = 1.0 / jnp.sqrt(jnp.float32(Dm))
        A1 = jnp.einsum('bqd,bkd->bqk', Q1, K1) * s
        A2 = jnp.einsum('bqd,bkd->bqk', Q2, K2) * s
        A = jax.nn.softmax(A2, axis=-1) - alpha * jax.nn.softmax(A1, axis=-1)
        return jnp.einsum('bqk,bkd->bqd', A, V)

    def _L1_cond_ref(x, token_ids, shift_state, time_maa_k, time_maa_r, w_recept, w_key, w_value):
        import jax, jax.numpy as jnp
        import numpy as np
        HASH_PRIME = 5099
        MIN_CAPACITY = 4
        B, T, D = x.shape
        E = w_key.shape[0]
        N = B * T
        C = max(MIN_CAPACITY, N // E)
        xprev = jnp.concatenate([shift_state[:, None, :], x[:, :-1]], axis=1)
        dxprev = xprev - x
        xk = x + dxprev * time_maa_k
        xr = x + dxprev * time_maa_r
        e_idx = token_ids.reshape(N).astype(jnp.int32) * HASH_PRIME % E
        onehot = (e_idx[:, None] == jnp.arange(E, dtype=jnp.int32)[None, :]).astype(jnp.int32)
        pos = jnp.take_along_axis(jnp.cumsum(onehot, axis=0), e_idx[:, None], axis=1)[:, 0] - 1
        keep = pos < C
        slot = jnp.where(keep, e_idx * C + pos, E * C)
        xk_flat = xk.reshape(N, D)
        buf = jnp.zeros((E * C + 1, D), dtype=x.dtype).at[slot].set(xk_flat)
        expert_in = buf[:E * C].reshape(E, C, D)
        h = jnp.square(jax.nn.relu(jnp.einsum('ecd,edf->ecf', expert_in, w_key)))
        expert_out = jnp.einsum('ecf,efd->ecd', h, w_value)
        out_pad = jnp.concatenate([expert_out.reshape(E * C, D), jnp.zeros((1, D), dtype=x.dtype)], axis=0)
        y = out_pad[slot].reshape(B, T, D)
        r = jax.nn.sigmoid(jnp.einsum('btd,ed->bte', xr, w_recept))
        return r * y
    x = x + _L0_cond_ref(cond_1024, x, L0_cond_Wq1, L0_cond_bq1, L0_cond_Wq2, L0_cond_bq2, L0_cond_Wk1, L0_cond_bk1, L0_cond_Wk2, L0_cond_bk2, L0_cond_Wv, L0_cond_bv, L0_cond_alpha)
    x = x + _L1_cond_ref(x, itok_BxS_2_50255, cond_1024, L1_cond_time_maa_k, L1_cond_time_maa_r, L1_cond_w_recept, L1_cond_w_key, L1_cond_w_value)
    return x

_drawn_inputs = setup_inputs


def setup_inputs(seed=0):
    import zlib

    import numpy as np

    out = dict(_drawn_inputs(seed))
    spreads = {}
    factors = {'L0_cond_bq2': 64.0,
     'L0_cond_bk2': 64.0,
     'L0_cond_bv': 8.0,
     'L1_cond_time_maa_r': 8.0,
     'L1_cond_w_recept': 5.051}
    for name, (base, spread) in spreads.items():
        noise = np.random.default_rng([zlib.crc32(name.encode()), seed]).standard_normal(out[name].shape)
        drawn = base * np.exp(spread * noise) if base else spread * noise
        out[name] = jnp.asarray(drawn.astype(out[name].dtype))
    for name, factor in factors.items():
        out[name] = (out[name] * factor).astype(out[name].dtype)
    return out
```

```python
from contextlib import ExitStack

import concourse.bass as bass
from concourse import mybir

F32 = mybir.dt.float32
F32R = mybir.dt.float32r
I32 = mybir.dt.int32
U32 = mybir.dt.uint32
ACT = mybir.ActivationFunctionType
ALU = mybir.AluOpType
AX = mybir.AxisListType

P = 128
HASH_PRIME = 5099
MIN_CAPACITY = 4


def build(nc, A):
    B, S, D = A["x"].shape
    E, _, F = A["w_key"].shape
    N = B * S
    CAP = max(MIN_CAPACITY, N // E)
    DC = D // P
    J = S // P
    JH = J // 2
    SH = S // 2
    FC = F // P
    CT = CAP // P
    NT = B * J
    SCALE = 1.0 / float(D) ** 0.5
    RAW = 4
    UNITS = 8
    KU = UNITS // 2
    RES = 4
    assert (D, J, FC, CT, E) == (512, 8, 8, 2, 16)

    xk_dram = nc.dram_tensor("xk_slots", (2 * N, D), F32, kind="Internal").ap()
    y_dram = nc.dram_tensor("y_slots", (N + 1, D), F32, kind="Internal").ap()
    shift_dram = nc.dram_tensor("shifted", (B, P + 1, D), F32, kind="Internal").ap()
    crow_dram = nc.dram_tensor("cond_rows", (B, D), F32, kind="Internal").ap()
    x_v = A["x"].rearrange("b (p j) d -> b p (j d)", p=P)
    out_v = A["out"].rearrange("b (p j) d -> b p (j d)", p=P)
    wkey_v = A["w_key"].rearrange("e (c p) f -> e p c f", p=P)
    wval_v = A["w_value"].rearrange("e (k p) d -> e p k d", p=P)

    with ExitStack() as ctx:
        def sem(name):
            return ctx.enter_context(nc.semaphore(name))

        def alloc(stack):
            return lambda name, shape, dt: stack.enter_context(nc.sbuf_tensor(name, shape, dt))

        sb = alloc(ctx)
        ident = sb("ident", [P, P], F32)
        mean_w = sb("mean_w", [P, P], F32)
        mk_row = sb("mk_row", [P, D], F32)
        mr_row = sb("mr_row", [P, D], F32)
        scat_idx = sb("scat_idx", [P, NT], I32)
        gath_idx = sb("gath_idx", [P, NT], I32)
        idx_now = sb("idx_now", [P, J], I32)
        dx = sb("dx", [P, D], F32)
        xk = sb("xk", [P, 2, D], F32)
        b_row = sb("b_row", [P, D], F32)
        x_before = sb("x_before", [P, D], F32)
        alpha = sb("alpha", [P, 1], F32)
        u_col = sb("u_col", [P, DC, 2], F32)
        neg_max = sb("neg_max", [P, J], F32)
        row_sum = sb("row_sum", [P, J], F32)
        row_inv = sb("row_inv", [P, J], F32)

        with ExitStack() as room:
            sbs = alloc(room)
            wq_raw = sbs("wq_raw", [P, DC, D], F32)
            wk_raw = sbs("wk_raw", [P, DC, D], F32)
            wv2_raw = sbs("wv2_raw", [P, DC, D], F32)
            wqT_hi = sbs("wqT_hi", [P, DC, D], F32R)
            wqT_lo = sbs("wqT_lo", [P, DC, D], F32R)
            wkT_hi = sbs("wkT_hi", [P, DC, D], F32R)
            wkT_lo = sbs("wkT_lo", [P, DC, D], F32R)
        x1 = sb("x1", [P, NT * D], F32)

        with ExitStack() as room:
            sba = alloc(room)
            x_in = sba("x_in", [P, JH, D], F32)
            m_hi = sba("m_hi", [P, DC, D], F32R)
            m_lo = sba("m_lo", [P, DC, D], F32R)
            wv_hi = sba("wv_hi", [P, DC, D], F32R)
            wv_lo = sba("wv_lo", [P, DC, D], F32R)
            xT_hi = sba("xT_hi", [P, DC, S], F32R)
            xT_lo = sba("xT_lo", [P, DC, S], F32R)
            z_hi = sba("z_hi", [P, DC, SH], F32R)
            z_lo = sba("z_lo", [P, DC, SH], F32R)
            prob = sba("prob", [P, S], F32)
            pT_hi = sba("pT_hi", [P, J, P], F32R)
            pT_lo = sba("pT_lo", [P, J, P], F32R)
            with ExitStack() as inner:
                sbs = alloc(inner)
                wv1_raw = sbs("wv1_raw", [P, DC, D], F32)
                upper = sbs("upper", [P, P], F32)
                ones = sbs("ones", [P, P], F32)
                tok = sbs("tok", [P, NT], I32)
                e_int = sbs("e_int", [P, NT], I32)
                e_f = sbs("e_f", [P, NT], F32)
                own_i = sbs("own_i", [P, NT], I32)
                own_f = sbs("own_f", [P, NT], F32)
                onehot = sbs("onehot", [P, B, J, E], F32)
                rank = sbs("rank", [P, B, J, E], F32)
                tot = sbs("tot", [P, B, E], F32)
                earlier = sbs("earlier", [P, B, E], F32)
                pos = sbs("pos", [P, NT], F32)
                keep = sbs("keep", [P, NT], F32)
                slot = sbs("slot", [P, NT], F32)
                diff = sbs("diff", [P, NT], F32)
                cond4 = sbs("cond4", [B, D], F32)
                bq4 = sbs("bq4", [DC, P], F32)
                condT = sbs("condT", [P, DC, B], F32)
                bq_hi = sbs("bq_hi", [P, DC, 2], F32R)
                bq_lo = sbs("bq_lo", [P, DC, 2], F32R)
                bv4 = sbs("bv4", [B, D], F32)
                crow4 = sbs("crow4", [B, D], F32)
                rest = sbs("rest", [P, 1], F32)
            v_hi = sba("v_hi", [P, J, D], F32R)
            v_lo = sba("v_lo", [P, J, D], F32R)

        with ExitStack() as room:
            sbm = alloc(room)
            w_raw = sbm("w_raw", [P, RAW, 2 * D], F32)
            wu_hi = sbm("wu_hi", [P, UNITS, 2 * D], F32R)
            wu_lo = sbm("wu_lo", [P, UNITS, 2 * D], F32R)
            with ExitStack() as inner:
                sbf = alloc(inner)
                xrT_hi = sbf("xrT_hi", [P, 2, D], F32R)
                xrT_lo = sbf("xrT_lo", [P, 2, D], F32R)
            xe_hi = sbm("xe_hi", [P, DC, CAP], F32R)
            xe_lo = sbm("xe_lo", [P, DC, CAP], F32R)
            with ExitStack() as inner:
                wr_raw = alloc(inner)("wr_raw", [P, DC, D], F32)
            h_hi = sbm("h_hi", [P, FC, CAP], F32R)
            h_lo = sbm("h_lo", [P, FC, CAP], F32R)
            with ExitStack() as inner:
                xr = alloc(inner)("xr", [P, 2, D], F32)
            xrow = sbm("xrow", [P, CT, D], F32)
            relu = sbm("relu", [P, 2, CAP], F32)
            hsq = sbm("hsq", [P, 2, CAP], F32)
            y_out = sbm("y_out", [P, CT, D], F32)
            wrT_hi = sbm("wrT_hi", [P, DC, D], F32R)
            wrT_lo = sbm("wrT_lo", [P, DC, D], F32R)

        with ExitStack() as room:
            sbf = alloc(room)
            y_got = sbf("y_got", [P, J, D], F32)
            res = sbf("res", [P, RES, D], F32)
            gate = sbf("gate", [P, 4, D], F32)

        ps = ctx.enter_context(nc.psum_tensor("ps", [P, 8, 512], F32))
        score_ps = ps[:, 0:2, :].rearrange("p a n -> p (a n)")
        row_ps = ps[:, 5, :]

        def tr_bank(n):
            return ps[:, 2 + n % 3, :]

        def out_bank(n):
            return ps[:, 6 + n % 2, :]

        ld_wq, ld_wk, ld_x, ld_wv2, ld_wv1 = (sem(n) for n in ("ld_wq", "ld_wk", "ld_x", "ld_wv2", "ld_wv1"))
        ld_tok, ld_small, ld_x1, ld_brow, ld_wr, ld_before = (
            sem(n) for n in ("ld_tok", "ld_small", "ld_x1", "ld_brow", "ld_wr", "ld_before"))
        ld_raw = [sem(f"ld_raw{i}") for i in range(RAW)]
        ld_xrow = sem("ld_xrow")
        consts_ok, own_ok, tot_ok, earlier_done, index_ok = (
            sem(n) for n in ("consts_ok", "own_ok", "tot_ok", "earlier_done", "index_ok"))
        mean_ok, wv_hi_ok, wv_lo_ok, crow_ok, crow_stored = (
            sem(n) for n in ("mean_ok", "wv_hi_ok", "wv_lo_ok", "crow_ok", "crow_stored"))
        zeroed, zero_row, cond_rows = sem("zeroed"), sem("zero_row"), sem("cond_rows")
        tr_done, tr_hi, tr_lo = sem("tr_done"), sem("tr_hi"), sem("tr_lo")
        out_done, out_hi, out_free = sem("out_done"), sem("out_hi"), sem("out_free")
        s_done, max_done, exp_done = sem("s_done"), sem("max_done"), sem("exp_done")
        row_done, row_ok, x1_ok = sem("row_done"), sem("row_ok"), sem("x1_ok")
        shift_out, shift_in = sem("shift_out"), sem("shift_in")
        scattered = [sem(f"scattered{i}") for i in range(2)]
        t_done, t_hi, t_lo = sem("t_done"), sem("t_hi"), sem("t_lo")
        v_used, w_hi, w_lo = sem("v_used"), sem("w_hi"), sem("w_lo")
        h_done, relu_ok, h_hi_ok, h_lo_ok = sem("h_done"), sem("relu_ok"), sem("h_hi_ok"), sem("h_lo_ok")
        y_done, y_copied = sem("y_done"), sem("y_copied")
        y_stored = [sem(f"y_stored{i}") for i in range(CT)]
        xr_ok, g_t_done, g_t_hi, g_t_lo = sem("xr_ok"), sem("g_t_done"), sem("g_t_hi"), sem("g_t_lo")
        g_done, gate_ok, res_ok = sem("g_done"), sem("gate_ok"), sem("res_ok")
        y_here = [sem(f"y_here{i}") for i in range(J)]
        stored = [sem(f"stored{i}") for i in range(RES)]
        settled = sem("settled")
        dve_chain, pool_chain = sem("dve_chain"), sem("pool_chain")
        inv_ok, xr_sub, xr_mul = sem("inv_ok"), sem("xr_sub"), sem("xr_mul")
        vsum_step, xk_step, idx_copied, hsq_ok, scaled = (
            sem(n) for n in ("vsum_step", "xk_step", "idx_copied", "hsq_ok", "scaled"))

        TR0, OUT0, HI0 = 9, 6, 4

        def TR(b, k):
            return TR0 + (8 + 2 * J) * b + k

        def OUT(b, k):
            return OUT0 + 24 * b + k

        def PV(b, i):
            return OUT(b, 12 + i if i < 3 else 16 + i)

        def HI(b, k):
            return HI0 + 16 * b + k

        def W(e, u):
            return UNITS * e + u

        def MT(e, g):
            return DC + 2 * e + g

        def tile(b, j):
            return x1[:, bass.ds((b * J + j) * D, D)]

        def batch_of(view, b):
            return view[b] if isinstance(b, int) else view[bass.ds(b, 1)].rearrange("a p n -> (a p) n")

        block = ctx.enter_context(nc.Block())

        @block.sync
        def _(sp):
            x_in_flat = x_in[:].rearrange("p j d -> p (j d)")
            sp.dma_start(tok[:].rearrange("p (b j) -> p b j", b=B),
                         A["tok"].rearrange("b (p j) -> p b j", p=P)).then_inc(ld_tok, 16)
            sp.dma_start(wq_raw[:], A["Wq2"].rearrange("(c p) e -> p c e", p=P)).then_inc(ld_wq, 16)
            sp.dma_start(wk_raw[:], A["Wk2"].rearrange("(c p) e -> p c e", p=P)).then_inc(ld_wk, 16)
            sp.dma_start(x_in_flat, x_v[0][:, 0:JH * D]).then_inc(ld_x, 16)
            sp.dma_start(wv2_raw[:], A["Wv"][D:2 * D, :].rearrange("(c p) e -> p c e", p=P)).then_inc(ld_wv2, 16)
            sp.dma_start(wv1_raw[:], A["Wv"][0:D, :].rearrange("(c p) e -> p c e", p=P)).then_inc(ld_wv1, 16)

            def load_half(b, h, after):
                sp.wait_ge(tr_done, after + 1)
                sp.dma_start(x_in_flat, batch_of(x_v, b)[:, h * JH * D:(h + 1) * JH * D]).then_inc(ld_x, 16)

            def load_residual(b):
                sp.dma_start(x1[:, bass.ds(b * J * D, J * D)], batch_of(x_v, b)).then_inc(ld_x1, 16)

            def load_row(b):
                sp.dma_start(b_row[:], crow_dram[bass.ds(b, 1), :].partition_broadcast(P)).then_inc(ld_brow, 16)

            load_half(0, 1, TR(0, 3))
            load_half(1, 0, TR(0, 7))
            sp.wait_ge(crow_ok, 1)
            sp.wait_ge(wv_hi_ok, 1)
            sp.wait_ge(wv_lo_ok, 1)
            load_residual(0)
            sp.dma_start(crow_dram, crow4[:]).then_inc(crow_stored, 16)
            sp.wait_ge(crow_stored, 16)
            load_row(0)
            sp.wait_ge(consts_ok, 1)
            sp.dma_start(xk_dram[0:N, :].rearrange("(p r) d -> p r d", p=P),
                         dx[:].unsqueeze(1).broadcast_to((P, N // P, D))).then_inc(zeroed, 16)

            def batch_loads(b, last):
                load_half(b, 1, TR(b, 3))
                if not last:
                    load_half(b + 1, 0, TR(b, 7))
                sp.wait_ge(ld_x1, 16 * b)
                load_residual(b)
                sp.wait_ge(x1_ok, J * b)
                load_row(b)

            with sp.Fori(1, B - 1) as b:
                batch_loads(b, False)
            batch_loads(B - 1, True)

            def load_unit(e, u):
                if u < KU:
                    src = wkey_v[bass.ds(e, 1), :, :, u * CAP:(u + 1) * CAP].rearrange("a p c f -> (a p) c f")
                    dst = w_raw[:, u % RAW, :].rearrange("p (c f) -> p c f", c=DC)
                else:
                    v = 2 * (u - KU)
                    src = wval_v[bass.ds(e, 1), :, v:v + 2, :].rearrange("a p k d -> (a p) k d")
                    dst = w_raw[:, u % RAW, :].rearrange("p (k d) -> p k d", k=2)
                sp.dma_start(dst, src).then_inc(ld_raw[u % RAW], 16)

            def load_rows(e):
                sp.dma_start(xrow[:], xk_dram[bass.ds(e * CAP, CAP), :].rearrange("(t p) d -> p t d", p=P)
                             ).then_inc(ld_xrow, 16)

            sp.wait_ge(out_done, OUT(B - 1, 18) + 1)
            for u in range(RAW):
                load_unit(0, u)
            sp.wait_ge(out_done, OUT(B - 1, 23) + 1)
            sp.dma_start(wr_raw[:], A["w_recept"].rearrange("(c p) d -> p c d", p=P)).then_inc(ld_wr, 16)
            for q in scattered:
                sp.wait_ge(q, 16 * NT // 2)
            load_rows(0)

            def expert_loads(e, first, last):
                for u in range(RAW if first else 0, UNITS):
                    sp.wait_ge(w_lo, W(e, u) - RAW + 1)
                    load_unit(e, u)
                if not last:
                    sp.wait_ge(t_done, MT(e, 1) + 1)
                    load_rows(e + 1)

            expert_loads(0, True, False)
            with sp.Fori(1, E - 1) as e:
                expert_loads(e, False, False)
            expert_loads(E - 1, False, True)

            def load_before(b):
                sp.dma_start(x_before[:], batch_of(shift_dram[:, 0:P, :], b)).then_inc(ld_before, 16)

            def batch_results(b, last):
                for j in range(J):
                    sp.wait_ge(res_ok, b * J + j + 1)
                    sp.dma_start(batch_of(out_v, b)[:, j * D:(j + 1) * D], res[:, j % RES, :]
                                 ).then_inc(stored[j % RES], 16)
                    if j == 0 and not last:
                        load_before(b + 1)

            load_before(0)
            with sp.Fori(0, B - 1) as b:
                batch_results(b, False)
            batch_results(B - 1, True)
            for q in stored:
                sp.wait_ge(q, 16 * NT // RES)

        @block.scalar
        def _(act):
            def hi(out, in_, done, bias=0.0, scale=1.0, func=ACT.Copy):
                nc.scalar.activation(out, in_, func, bias=bias, scale=scale).then_inc(done, 1)

            def tr_split(n, out):
                act.wait_ge(tr_done, n + 1)
                hi(out, tr_bank(n), tr_hi)

            act.wait_ge(tr_done, 1)
            for k in range(2):
                op = nc.scalar.activation(bq_hi[:, :, k], tr_bank(0)[:, 0:DC], ACT.Copy)
            op.then_inc(tr_hi, 1)
            for k in range(2 * DC):
                tr_split(1 + k, (wqT_hi, wkT_hi)[k // DC][:, k % DC, :])
            act.wait_ge(ld_wv2, 16)
            nc.scalar.activation(wv_hi[:].rearrange("p c n -> p (c n)"), wv2_raw[:].rearrange("p c n -> p (c n)"),
                                 ACT.Copy).then_inc(wv_hi_ok, 1)
            for k in range(DC):
                act.wait_ge(out_done, k + 1)
                hi(m_hi[:, k, :], out_bank(k), out_hi, scale=SCALE)

            def z_split(b, k0):
                for c in range(DC):
                    act.wait_ge(out_done, OUT(b, k0 + c) + 1)
                    hi(z_hi[:, c, :], out_bank(OUT0 + k0 + c), out_hi, bias=u_col[:, c, 0:1], func=ACT.Identity)

            def batch(b, first):
                for h in range(2):
                    for c in range(DC):
                        act.wait_ge(tr_done, TR(b, DC * h + c) + 1)
                        hi(xT_hi[:, c, h * SH:(h + 1) * SH], tr_bank(TR0 + DC * h + c), tr_hi)
                if first:
                    act.wait_ge(crow_ok, 1)
                    act.wait_ge(crow_stored, 16)
                z_split(b, 0)
                for i in range(J):
                    act.wait_ge(max_done, b * J + i + 1)
                    nc.scalar.activation(prob[:], score_ps, ACT.Exp, bias=neg_max[:, i:i + 1],
                                         accum_out=row_sum[:, i:i + 1]).then_inc(exp_done, 1)
                    if i == 0:
                        for j in range(J):
                            act.wait_ge(out_done, OUT(b, DC + j) + 1)
                            if j == 0:
                                act.wait_ge(vsum_step, (2 * J - 1) * b)
                            hi(v_hi[:, j, :], out_bank(OUT0 + DC + j), out_hi)
                    for g in range(2):
                        act.wait_ge(tr_done, TR(b, 8 + 2 * i + g) + 1)
                        hi(pT_hi[:, JH * g:JH * (g + 1), :].rearrange("p a n -> p (a n)"),
                           tr_bank(TR0 + 8 + 2 * i + g), tr_hi)
                    if i == JH - 1:
                        z_split(b, 15)

            batch(0, True)
            with act.Fori(1, B) as b:
                batch(b, False)

            def unit_split(e, u, first):
                act.wait_ge(ld_raw[u % RAW], 16 * (2 * e + u // RAW + 1))
                if first:
                    act.wait_ge(tr_done, TR(B - 1, 23) + 1)
                else:
                    if u < KU:
                        act.wait_ge(h_done, FC * (e - 1) + 2 * u + 2)
                    elif u < UNITS - 1:
                        act.wait_ge(v_used, (KU - 1) * (e - 1) + u - KU + 1)
                    else:
                        act.wait_ge(y_done, CT * e)
                hi(wu_hi[:, u, :], w_raw[:, u % RAW, :], w_hi)

            def rows_split(e):
                for g in range(2):
                    act.wait_ge(t_done, MT(e, g) + 1)
                    hi(xe_hi[:, 2 * g:2 * g + 2, :].rearrange("p a n -> p (a n)"), ps[:, g, :], t_hi)

            def copy_y(e):
                for t in range(CT):
                    act.wait_ge(y_done, CT * e + t + 1)
                    act.wait_ge(y_stored[t], 16 * e)
                    nc.scalar.activation(y_out[:, t, :], ps[:, 6 + t, :], ACT.Copy).then_inc(y_copied, 1)

            def hidden(e, first):
                for f in range(FC):
                    act.wait_ge(h_done, FC * e + f + 1)
                    if not (first and f < 2):
                        act.wait_ge(h_lo_ok, FC * e + f - 1)
                    nc.scalar.activation(relu[:, f % 2, :], ps[:, 2 + f % 4, 0:CAP], ACT.Relu).then_inc(relu_ok, 1)
                    act.wait_ge(relu_ok, FC * e + f + 1)
                    nc.scalar.activation(h_hi[:, f, :], relu[:, f % 2, :], ACT.Square).then_inc(h_hi_ok, 1)
                    if f % 2:
                        unit_split(e, KU + f // 2, first)

            for u in range(KU):
                unit_split(0, u, True)
            act.wait_ge(vsum_step, (2 * J - 1) * B)
            for g in range(DC):
                act.wait_ge(t_done, g + 1)
                hi(wrT_hi[:, g, :], ps[:, g % 2, :], t_hi)
            rows_split(0)
            hidden(0, True)
            with act.Fori(1, E) as e:
                rows_split(e)
                for u in range(KU):
                    unit_split(e, u, False)
                copy_y(e - 1)
                hidden(e, False)

            def gate_split(n, k, first):
                act.wait_ge(g_t_done, n + 1)
                if not (first and k < 2):
                    act.wait_ge(g_done, n - 1)
                hi(xrT_hi[:, k % 2, :], ps[:, k % 2, :], g_t_hi)

            def sigmoid(n, k, first):
                act.wait_ge(g_done, n + 1)
                if not first:
                    act.wait_ge(res_ok, n - 3)
                nc.scalar.activation(gate[:, k % 4, :], ps[:, 6 + k % 2, :], ACT.Sigmoid).then_inc(gate_ok, 1)

            gate_split(0, 0, True)
            copy_y(E - 1)
            for k in range(1, 4):
                gate_split(k, k, True)
                sigmoid(k - 1, k - 1, True)
            with act.Fori(1, NT // 4) as q:
                for k in range(4):
                    gate_split(4 * q + k, k, False)
                    sigmoid(4 * q + k - 1, (k - 1) % 4, False)
            sigmoid(NT - 1, 3, False)

        @block.vector
        def _(dve):
            chain = [0]

            def link(op):
                chain[0] += 1
                op.then_inc(dve_chain, 1)
                dve.wait_ge(dve_chain, chain[0])

            tt, ts, stt = nc.vector.tensor_tensor, nc.vector.tensor_scalar, nc.vector.scalar_tensor_tensor

            def lo(out, in_, hi_part, done):
                tt(out, in_, hi_part.bitcast(F32), ALU.subtract).then_inc(done, 1)

            dve.wait_ge(ld_tok, 16)
            link(ts(e_int[:], tok[:], E - 1, None, ALU.bitwise_and))
            link(ts(tok[:], e_int[:], float(HASH_PRIME % E), None, ALU.mult))
            link(ts(e_int[:], tok[:], E - 1, None, ALU.bitwise_and))
            link(nc.vector.tensor_copy(e_f[:], e_int[:]))
            oh = onehot[:].rearrange("p b j e -> p (b j) e")
            for e in range(E):
                op = ts(oh[:, :, e], e_f[:], float(e), None, ALU.is_equal)
            link(op)
            link(nc.vector.tensor_reduce(tot[:], onehot[:].rearrange("p b j e -> p b e j"), AX.X, ALU.add))
            link(nc.vector.memset(earlier[:], 0.0))
            for b in range(1, B - 1):
                link(tt(earlier[:, b, :], earlier[:, b - 1, :], tot[:, b - 1, :], ALU.add))
            tt(earlier[:, B - 1, :], earlier[:, B - 2, :], tot[:, B - 2, :], ALU.add).then_inc(tot_ok, 1)
            dve.wait_ge(earlier_done, 1)
            link(nc.vector.tensor_copy(rank[:, :, 0, :], row_ps[:, 0:B * E].rearrange("p (b e) -> p b e", b=B)))
            for j in range(1, J):
                link(tt(rank[:, :, j, :], rank[:, :, j - 1, :], onehot[:, :, j - 1, :], ALU.add))
            rank_f = rank[:].rearrange("p b j e -> p (b j e)")
            link(tt(rank_f, rank_f, onehot[:].rearrange("p b j e -> p (b j e)"), ALU.mult))
            link(nc.vector.tensor_reduce(pos[:], rank[:].rearrange("p b j e -> p (b j) e"), AX.X, ALU.add))
            link(ts(keep[:], pos[:], float(CAP), None, ALU.is_lt))
            link(stt(slot[:], e_f[:], float(CAP), pos[:], ALU.mult, ALU.add))
            dve.wait_ge(own_ok, 1)
            link(nc.vector.tensor_copy(own_f[:], own_i[:]))
            link(tt(diff[:], slot[:], own_f[:], ALU.subtract))
            link(tt(diff[:], diff[:], keep[:], ALU.mult))
            link(tt(scat_idx[:], diff[:], own_f[:], ALU.add))
            link(ts(diff[:], slot[:], float(-N), None, ALU.add))
            link(tt(diff[:], diff[:], keep[:], ALU.mult))
            ts(gath_idx[:], diff[:], float(N), None, ALU.add).then_inc(index_ok, 1)

            dve.wait_ge(ld_small, 16 * 6)
            dve.wait_ge(consts_ok, 1)
            link(ts(rest[:], alpha[:], -1.0, 1.0, ALU.mult, ALU.add))
            ts(mean_w[:], mean_w[:], alpha[:], None, ALU.mult).then_inc(mean_ok, 1)
            dve.wait_ge(tr_hi, 1)
            for k in range(2):
                tt(bq_lo[:, :, k], tr_bank(0)[:, 0:DC], bq_hi[:, :, k].bitcast(F32), ALU.subtract)
            nc.vector.tensor_copy(condT[:].rearrange("p c b -> p (c b)"), tr_bank(0)[:, DC:DC + DC * B]
                                  ).then_inc(tr_lo, 1)
            for k in range(2 * DC):
                dve.wait_ge(tr_hi, k + 2)
                lo((wqT_lo, wkT_lo)[k // DC][:, k % DC, :], tr_bank(1 + k), (wqT_hi, wkT_hi)[k // DC][:, k % DC, :], tr_lo)
            dve.wait_ge(wv_hi_ok, 1)
            lo(wv_lo[:].rearrange("p c n -> p (c n)"), wv2_raw[:].rearrange("p c n -> p (c n)"),
               wv_hi[:].rearrange("p c n -> p (c n)"), wv_lo_ok)
            for k in range(DC):
                dve.wait_ge(out_hi, k + 1)
                stt(m_lo[:, k, :], out_bank(k), SCALE, m_hi[:, k, :].bitcast(F32), ALU.mult, ALU.subtract
                    ).then_inc(out_free, 1)
            dve.wait_ge(out_done, 5)
            ts(u_col[:].rearrange("p c k -> p (c k)"), out_bank(4)[:, 0:2 * DC], SCALE, None, ALU.mult
               ).then_inc(out_free, 1)
            dve.wait_ge(out_done, 6)
            tt(crow4[:], out_bank(5)[0:B, :], bv4[:], ALU.add).then_inc(out_free, 1)
            dve.wait_ge(out_free, 6)
            ts(crow4[:], crow4[:], rest[0:B, :], None, ALU.mult).then_inc(crow_ok, 1)

            def pv_evacuate(b, i):
                dve.wait_ge(out_done, PV(b, i) + 1)
                dve.wait_ge(ld_x1, 16 * (b + 1))
                dve.wait_ge(inv_ok, b * J + i + 1)
                stt(tile(b, i), out_bank(PV(0, i)), row_inv[:, i:i + 1], tile(b, i), ALU.mult, ALU.add
                    ).then_inc(out_free, 1)

            def z_split(b, k0, h0):
                for c in range(DC):
                    dve.wait_ge(out_hi, HI(b, h0 + c) + 1)
                    stt(z_lo[:, c, :], out_bank(OUT0 + k0 + c), u_col[:, c, 0:1], z_hi[:, c, :].bitcast(F32),
                        ALU.add, ALU.subtract).then_inc(out_free, 1)

            def batch(b, first):
                for h in range(2):
                    for c in range(DC):
                        dve.wait_ge(tr_hi, TR(b, DC * h + c) + 1)
                        lo(xT_lo[:, c, h * SH:(h + 1) * SH], tr_bank(TR0 + DC * h + c),
                           xT_hi[:, c, h * SH:(h + 1) * SH], tr_lo)
                    if h == 0 and not first:
                        pv_evacuate(b - 1, J - 1)
                z_split(b, 0, 0)
                for i in range(J):
                    dve.wait_ge(s_done, b * J + i + 1)
                    nc.vector.tensor_reduce(neg_max[:, i:i + 1], score_ps, AX.X, ALU.max, negate=True
                                            ).then_inc(max_done, 1)
                    if i == 0:
                        for j in range(J):
                            dve.wait_ge(out_hi, HI(b, DC + j) + 1)
                            lo(v_lo[:, j, :], out_bank(OUT0 + DC + j), v_hi[:, j, :], out_free)
                    else:
                        pv_evacuate(b, i - 1)
                    if i == 3:
                        dve.wait_ge(row_done, b + 1)
                        dve.wait_ge(ld_brow, 16 * (b + 1))
                        tt(b_row[:], row_ps, b_row[:], ALU.add).then_inc(row_ok, 1)
                    dve.wait_ge(exp_done, b * J + i + 1)
                    nc.vector.reciprocal(row_inv[:, i:i + 1], row_sum[:, i:i + 1]).then_inc(inv_ok, 1)
                    for g in range(2):
                        dve.wait_ge(tr_hi, TR(b, 8 + 2 * i + g) + 1)
                        lo(pT_lo[:, JH * g:JH * (g + 1), :].rearrange("p a n -> p (a n)"),
                           tr_bank(TR0 + 8 + 2 * i + g),
                           pT_hi[:, JH * g:JH * (g + 1), :].rearrange("p a n -> p (a n)"), tr_lo)
                    if i == JH - 1:
                        z_split(b, 15, 12)

            batch(0, True)
            with dve.Fori(1, B) as b:
                batch(b, False)
            pv_evacuate(B - 1, J - 1)

            def unit_split(e, u):
                dve.wait_ge(w_hi, W(e, u) + 1)
                lo(wu_lo[:, u, :], w_raw[:, u % RAW, :], wu_hi[:, u, :], w_lo)

            def rows_split(e):
                for g in range(2):
                    dve.wait_ge(t_hi, MT(e, g) + 1)
                    lo(xe_lo[:, 2 * g:2 * g + 2, :].rearrange("p a n -> p (a n)"), ps[:, g, :],
                       xe_hi[:, 2 * g:2 * g + 2, :].rearrange("p a n -> p (a n)"), t_lo)

            for u in range(KU):
                unit_split(0, u)
            for g in range(DC):
                dve.wait_ge(t_hi, g + 1)
                lo(wrT_lo[:, g, :], ps[:, g % 2, :], wrT_hi[:, g, :], t_lo)
            rows_split(0)
            for u in range(KU, UNITS):
                unit_split(0, u)
            with dve.Fori(1, E) as e:
                rows_split(e)
                for u in range(UNITS):
                    unit_split(e, u)

            def shifted_rows(b, j, first):
                n = b * J + j
                if first and j < 2:
                    dve.wait_ge(t_done, MT(E - 1, 1) + 1)
                else:
                    dve.wait_ge(g_t_done, n - 1)
                if first and j == 0:
                    dve.wait_ge(x1_ok, NT)
                if j == 0:
                    dve.wait_ge(ld_before, 16 * (b + 1))
                before = x_before[:] if j == 0 else tile(b, j - 1)
                row = xr[:, j % 2, :]
                tt(row, before, tile(b, j), ALU.subtract).then_inc(xr_sub, 1)
                dve.wait_ge(xr_sub, n + 1)
                tt(row, row, mr_row[:], ALU.mult).then_inc(xr_mul, 1)
                dve.wait_ge(xr_mul, n + 1)
                tt(row, row, tile(b, j), ALU.add).then_inc(xr_ok, 1)

            def gate_split(n, k):
                dve.wait_ge(g_t_hi, n + 1)
                lo(xrT_lo[:, k % 2, :], ps[:, k % 2, :], xrT_hi[:, k % 2, :], g_t_lo)

            for j in range(J):
                shifted_rows(0, j, True)
                if j:
                    gate_split(j - 1, j - 1)
            with dve.Fori(1, B) as b:
                for j in range(J):
                    shifted_rows(b, j, False)
                    gate_split(b * J + j - 1, (j - 1) % 2)
            gate_split(NT - 1, 1)

        @block.gpsimd
        def _(pool):
            chain = [0]

            def link(op):
                chain[0] += 1
                op.then_inc(pool_chain, 1)
                pool.wait_ge(pool_chain, chain[0])

            def settle():
                pool.sem_inc(settled, 1)

            tt = nc.gpsimd.tensor_tensor
            for dst, src in ((bq4[:], A["bq2"].rearrange("(c p) -> c p", p=P)),
                             (cond4[:], A["cond"]),
                             (bv4[:], A["bv"].rearrange("(a d) -> a d", a=1).partition_broadcast(B)),
                             (alpha[:], A["alpha"].rearrange("(a d) -> a d", a=1).partition_broadcast(P)),
                             (mk_row[:], A["mk"].rearrange("(a d) -> a d", a=1).partition_broadcast(P)),
                             (mr_row[:], A["mr"].rearrange("(a d) -> a d", a=1).partition_broadcast(P))):
                pool.dma_start(dst, src).then_inc(ld_small, 16)
            link(nc.gpsimd.memset(ident[:], 0.0))
            link(nc.gpsimd.affine_select(out=ident[:], in_=ident[:], compare_op=ALU.not_equal, fill=1.0, base=0,
                                         pattern=[[-1, P]], channel_multiplier=1))
            link(nc.gpsimd.memset(upper[:], 1.0))
            link(nc.gpsimd.affine_select(out=upper[:], in_=upper[:], compare_op=ALU.is_gt, fill=0.0, base=0,
                                         pattern=[[1, P]], channel_multiplier=-1))
            link(nc.gpsimd.memset(ones[:], 1.0))
            link(nc.gpsimd.memset(dx[:], 0.0))
            nc.gpsimd.memset(mean_w[:], -1.0 / S).then_inc(consts_ok, 1)
            nc.gpsimd.iota(own_i[:].rearrange("p (b j) -> p b j", b=B), [[S, B], [1, J]], base=N,
                           channel_multiplier=J).then_inc(own_ok, 1)
            pool.dma_start(shift_dram[:, 0, :], A["cond"]).then_inc(cond_rows, 16)
            pool.dma_start(y_dram[N:N + 1, :], dx[0:1, :]).then_inc(zero_row, 16)
            pool.wait_ge(zeroed, 16)
            pool.wait_ge(zero_row, 16)
            pool.wait_ge(cond_rows, 16)

            def x1_tile(b, j):
                pool.wait_ge(out_free, PV(b, j) + 1)
                pool.wait_ge(row_ok, b + 1)
                settle()
                tt(tile(b, j), tile(b, j), b_row[:], ALU.add).then_inc(x1_ok, 1)
                pool.wait_ge(x1_ok, b * J + j + 1)

            def xk_tile(b, k, j, before):
                step = 3 * (b * J + k)
                settle()
                tt(dx[:], before, tile(b, j), ALU.subtract).then_inc(xk_step, 1)
                pool.wait_ge(xk_step, step + 1)
                tt(dx[:], dx[:], mk_row[:], ALU.mult).then_inc(xk_step, 1)
                pool.wait_ge(xk_step, step + 2)
                pool.wait_ge(scattered[k % 2], 16 * (b * (J // 2) + k // 2))
                settle()
                tt(xk[:, k % 2, :], dx[:], tile(b, j), ALU.add).then_inc(xk_step, 1)
                pool.wait_ge(xk_step, step + 3)
                settle()
                pool.indirect_dma_start(
                    out=xk_dram, out_offset=bass.IndirectOffsetOnAxis(ap=idx_now[:, j:j + 1].bitcast(U32), axis=0),
                    in_=xk[:, k % 2, :], in_offset=None).then_inc(scattered[k % 2], 16)

            def batch(b, first):
                if first:
                    pool.wait_ge(index_ok, 1)
                for q in scattered:
                    pool.wait_ge(q, 16 * (J // 2) * b)
                settle()
                nc.gpsimd.tensor_copy(idx_now[:], scat_idx[:, bass.ds(b * J, J)]).then_inc(idx_copied, 1)
                steps = 2 * J - 1
                if not first:
                    pool.wait_ge(row_done, b)
                pool.wait_ge(out_free, OUT(b, DC) + 1)
                tt(dx[:], v_hi[:, 0, :].bitcast(F32), v_lo[:, 0, :].bitcast(F32), ALU.add).then_inc(vsum_step, 1)
                for k in range(1, steps):
                    j = (k + 1) // 2
                    if k % 2:
                        pool.wait_ge(out_free, OUT(b, DC + j) + 1)
                    pool.wait_ge(vsum_step, steps * b + k)
                    tt(dx[:], dx[:], (v_hi, v_lo)[(k + 1) % 2][:, j, :].bitcast(F32), ALU.add).then_inc(vsum_step, 1)
                pool.wait_ge(idx_copied, b + 1)
                for j in range(J):
                    x1_tile(b, j)
                    if j == 0:
                        pool.wait_ge(row_done, b + 1)
                    else:
                        xk_tile(b, j - 1, j, tile(b, j - 1))
                settle()
                pool.dma_start(batch_of(shift_dram[:, 1:P + 1, :], b), tile(b, J - 1)).then_inc(shift_out, 16)
                pool.wait_ge(shift_out, 16 * (b + 1))
                settle()
                pool.dma_start(dx[:], batch_of(shift_dram[:, 0:P, :], b)).then_inc(shift_in, 16)
                pool.wait_ge(shift_in, 16 * (b + 1))
                xk_tile(b, J - 1, 0, dx[:])

            batch(0, True)
            with pool.Fori(1, B) as b:
                batch(b, False)

            def hidden(e, first):
                for f in range(FC):
                    n = FC * e + f
                    pool.wait_ge(relu_ok, n + 1)
                    tt(hsq[:, f % 2, :], relu[:, f % 2, :], relu[:, f % 2, :], ALU.mult).then_inc(hsq_ok, 1)
                    pool.wait_ge(hsq_ok, n + 1)
                    pool.wait_ge(h_hi_ok, n + 1)
                    tt(h_lo[:, f, :], hsq[:, f % 2, :], h_hi[:, f, :].bitcast(F32), ALU.subtract
                       ).then_inc(h_lo_ok, 1)

            def store_y(e):
                for t in range(CT):
                    pool.wait_ge(y_copied, CT * e + t + 1)
                    settle()
                    pool.dma_start(y_dram[bass.ds(e * CAP + t * P, P), :], y_out[:, t, :]).then_inc(y_stored[t], 16)

            hidden(0, True)
            with pool.Fori(1, E) as e:
                store_y(e - 1)
                hidden(e, False)
            store_y(E - 1)

            def indices(b):
                settle()
                nc.gpsimd.tensor_copy(idx_now[:], gath_idx[:, bass.ds(b * J, J)]).then_inc(idx_copied, 1)
                pool.wait_ge(idx_copied, B + b + 1)
                settle()

            def gather(j):
                pool.indirect_dma_start(
                    out=y_got[:, j, :], out_offset=None, in_=y_dram,
                    in_offset=bass.IndirectOffsetOnAxis(ap=idx_now[:, j:j + 1].bitcast(U32), axis=0)
                ).then_inc(y_here[j], 16)

            for q in scattered:
                pool.wait_ge(q, 16 * NT // 2)
            for q in y_stored:
                pool.wait_ge(q, 16 * E)
            indices(0)
            for j in range(J):
                gather(j)

            def batch_results(b, first, last):
                if not last:
                    for j in range(J):
                        pool.wait_ge(y_here[j], 16 * (b + 1))
                    indices(b + 1)
                for j in range(J):
                    n = b * J + j
                    if last:
                        pool.wait_ge(y_here[j], 16 * (b + 1))
                    pool.wait_ge(gate_ok, n + 1)
                    tt(y_got[:, j, :], y_got[:, j, :], gate[:, j % 4, :], ALU.mult).then_inc(scaled, 1)
                    pool.wait_ge(scaled, n + 1)
                    if not (first and j < RES):
                        pool.wait_ge(stored[j % RES], 16 * (b * (J // RES) + j // RES))
                    settle()
                    tt(res[:, j % RES, :], y_got[:, j, :], tile(b, j), ALU.add).then_inc(res_ok, 1)
                    if not last:
                        pool.wait_ge(res_ok, n + 1)
                        settle()
                        gather(j)

            batch_results(0, True, False)
            with pool.Fori(1, B - 1) as b:
                batch_results(b, False, False)
            batch_results(B - 1, False, True)

        @block.tensor
        def _(pe):
            def mm3(out, l_hi, l_lo, r_hi, r_lo, start, stop):
                nc.tensor.matmul(out, l_hi, r_hi, start=start, stop=False)
                nc.tensor.matmul(out, l_hi, r_lo, start=False, stop=False)
                return nc.tensor.matmul(out, l_lo, r_hi, start=False, stop=stop)

            pe.wait_ge(consts_ok, 1)
            pe.wait_ge(tot_ok, 1)
            counts = row_ps[:, 0:B * E]
            nc.tensor.matmul(counts, upper[:], tot[:].rearrange("p b e -> p (b e)"), start=True, stop=False)
            nc.tensor.matmul(counts, ones[:], earlier[:].rearrange("p b e -> p (b e)"), start=False, stop=True
                             ).then_inc(earlier_done, 1)
            pe.wait_ge(ld_small, 16 * 6)
            nc.tensor.transpose(tr_bank(0)[:, 0:DC], bq4[:], ident[0:DC, 0:DC])
            for c in range(DC):
                op = nc.tensor.transpose(tr_bank(0)[:, DC + c * B:DC + (c + 1) * B], cond4[:, c * P:(c + 1) * P],
                                         ident[0:B, 0:B])
            op.then_inc(tr_done, 1)
            for k in range(2 * DC):
                if k % DC == 0:
                    pe.wait_ge((ld_wq, ld_wk)[k // DC], 16)
                if 1 + k >= 3:
                    pe.wait_ge(tr_lo, k - 1)
                raw = (wq_raw, wk_raw)[k // DC]
                for c in range(DC):
                    op = nc.tensor.transpose(tr_bank(1 + k)[:, c * P:(c + 1) * P],
                                             raw[:, c, (k % DC) * P:(k % DC + 1) * P], ident[:])
                op.then_inc(tr_done, 1)
            pe.wait_ge(tr_lo, TR0)
            for t in range(DC):
                if t >= 2:
                    pe.wait_ge(out_free, t - 1)
                for c in range(DC):
                    op = mm3(out_bank(t), wqT_hi[:, c, t * P:(t + 1) * P], wqT_lo[:, c, t * P:(t + 1) * P],
                             wkT_hi[:, c, :], wkT_lo[:, c, :], c == 0, c == DC - 1)
                op.then_inc(out_done, 1)
            pe.wait_ge(out_free, 3)
            for t in range(DC):
                for c in range(DC):
                    op = mm3(out_bank(4)[:, 2 * t:2 * t + 2], wkT_hi[:, c, t * P:(t + 1) * P],
                             wkT_lo[:, c, t * P:(t + 1) * P], bq_hi[:, c, :], bq_lo[:, c, :], c == 0, c == DC - 1)
            op.then_inc(out_done, 1)
            pe.wait_ge(out_free, 4)
            pe.wait_ge(ld_wv1, 16)
            for c in range(DC):
                op = nc.tensor.matmul(out_bank(5)[0:B, :], condT[:, c, :], wv1_raw[:, c, :],
                                      start=(c == 0), stop=(c == DC - 1))
            op.then_inc(out_done, 1)

            def transpose_x(b, h):
                for c in range(DC):
                    if c == 0:
                        pe.wait_ge(ld_x, 16 * (2 * b + h + 1))
                    pe.wait_ge(tr_lo, TR(b, DC * h + c) - 2)
                    for t in range(JH):
                        op = nc.tensor.transpose(tr_bank(TR0 + DC * h + c)[:, t * P:(t + 1) * P],
                                                 x_in[:, t, c * P:(c + 1) * P], ident[:])
                    op.then_inc(tr_done, 1)

            def z_tiles(b, h):
                k0 = 15 if h else 0
                pe.wait_ge(tr_lo, TR(b, DC * (h + 1) - 1) + 1)
                for t in range(DC):
                    pe.wait_ge(out_free, OUT(b, k0 + t) - 1)
                    for c in range(DC):
                        op = mm3(out_bank(OUT0 + k0 + t), m_hi[:, c, t * P:(t + 1) * P], m_lo[:, c, t * P:(t + 1) * P],
                                 xT_hi[:, c, h * SH:(h + 1) * SH], xT_lo[:, c, h * SH:(h + 1) * SH],
                                 c == 0, c == DC - 1)
                    op.then_inc(out_done, 1)

            def v_tiles(b):
                for j in range(J):
                    pe.wait_ge(out_free, OUT(b, DC + j) - 1)
                    for c in range(DC):
                        op = mm3(out_bank(OUT0 + DC + j), xT_hi[:, c, j * P:(j + 1) * P], xT_lo[:, c, j * P:(j + 1) * P],
                                 wv_hi[:, c, :], wv_lo[:, c, :], c == 0, c == DC - 1)
                    op.then_inc(out_done, 1)

            def scores(b, i):
                q = (i % JH) * P
                for k in range(2):
                    for c in range(DC):
                        if i % JH == 0 and k == 0:
                            pe.wait_ge(out_free, OUT(b, (15 if i else 0) + c) + 1)
                        if i == 0 and k == 1 and c == 0:
                            pe.wait_ge(tr_lo, TR(b, 2 * DC - 1) + 1)
                        op = mm3(ps[:, k, :], z_hi[:, c, q:q + P], z_lo[:, c, q:q + P],
                                 xT_hi[:, c, k * SH:(k + 1) * SH], xT_lo[:, c, k * SH:(k + 1) * SH],
                                 c == 0, c == DC - 1)
                op.then_inc(s_done, 1)

            def transpose_p(b, i):
                pe.wait_ge(exp_done, b * J + i + 1)
                for g in range(2):
                    pe.wait_ge(tr_lo, TR(b, 8 + 2 * i + g) - 2)
                    for t in range(JH):
                        k = JH * g + t
                        op = nc.tensor.transpose(tr_bank(TR0 + 8 + 2 * i + g)[:, t * P:(t + 1) * P],
                                                 prob[:, k * P:(k + 1) * P], ident[:])
                    op.then_inc(tr_done, 1)

            def values(b, i):
                pe.wait_ge(out_free, PV(b, i) - 1)
                for j in range(J):
                    if j % JH == 0:
                        pe.wait_ge(tr_lo, TR(b, 8 + 2 * i + j // JH) + 1)
                    if i == 0 and j == 0:
                        pe.wait_ge(out_free, OUT(b, 2 * DC + JH - 1) + 1)
                    op = mm3(out_bank(PV(0, i)), pT_hi[:, j, :], pT_lo[:, j, :], v_hi[:, j, :], v_lo[:, j, :],
                             j == 0, j == J - 1)
                op.then_inc(out_done, 1)

            def mean_row(b):
                pe.wait_ge(vsum_step, (2 * J - 1) * (b + 1))
                nc.tensor.matmul(row_ps, mean_w[:], dx[:], start=True, stop=True).then_inc(row_done, 1)

            def batch(b, first):
                transpose_x(b, 0)
                if not first:
                    values(b - 1, J - 1)
                transpose_x(b, 1)
                z_tiles(b, 0)
                scores(b, 0)
                v_tiles(b)
                transpose_p(b, 0)
                for i in range(1, J):
                    scores(b, i)
                    values(b, i - 1)
                    if i == 3:
                        mean_row(b)
                    transpose_p(b, i)
                    if i == JH - 1:
                        z_tiles(b, 1)

            pe.wait_ge(wv_lo_ok, 1)
            pe.wait_ge(mean_ok, 1)
            pe.wait_ge(earlier_done, 1)
            batch(0, True)
            with pe.Fori(1, B) as b:
                batch(b, False)
            values(B - 1, J - 1)

            pe.wait_ge(ld_wr, 16)
            pe.wait_ge(row_ok, B)
            for g in range(DC):
                if g >= 2:
                    pe.wait_ge(t_lo, g - 1)
                for c in range(DC):
                    op = nc.tensor.transpose(ps[:, g % 2, c * P:(c + 1) * P], wr_raw[:, c, g * P:(g + 1) * P], ident[:])
                op.then_inc(t_done, 1)

            def transpose_rows(e):
                pe.wait_ge(ld_xrow, 16 * (e + 1))
                for g in range(2):
                    pe.wait_ge(t_lo, MT(e, g) - 1)
                    for c in range(2):
                        for t in range(CT):
                            op = nc.tensor.transpose(ps[:, g, c * CAP + t * P:c * CAP + (t + 1) * P],
                                                     xrow[:, t, (2 * g + c) * P:(2 * g + c + 1) * P], ident[:])
                    op.then_inc(t_done, 1)

            def hidden(e, first):
                pe.wait_ge(t_lo, MT(e, 1) + 1)
                for f in range(FC):
                    u = f // 2
                    if f % 2 == 0:
                        pe.wait_ge(w_lo, W(e, u) + 1)
                    if not (first and f < 4):
                        pe.wait_ge(relu_ok, FC * e + f - 3)
                    for c in range(DC):
                        at = c * CAP + (f % 2) * P
                        op = mm3(ps[:, 2 + f % 4, 0:CAP], wu_hi[:, u, at:at + P], wu_lo[:, u, at:at + P],
                                 xe_hi[:, c, :], xe_lo[:, c, :], c == 0, c == DC - 1)
                    op.then_inc(h_done, 1)

            def expert_out(e):
                for t in range(CT):
                    for f in range(FC):
                        u = KU + f // 2
                        if t == 0:
                            pe.wait_ge(h_lo_ok, FC * e + f + 1)
                            if f % 2 == 0:
                                pe.wait_ge(w_lo, W(e, u) + 1)
                        at = (f % 2) * D
                        op = mm3(ps[:, 6 + t, :], h_hi[:, f, t * P:(t + 1) * P], h_lo[:, f, t * P:(t + 1) * P],
                                 wu_hi[:, u, at:at + D], wu_lo[:, u, at:at + D], f == 0, f == FC - 1)
                        if t == CT - 1 and f % 2 and f < FC - 1:
                            op.then_inc(v_used, 1)
                    op.then_inc(y_done, 1)

            pe.wait_ge(out_free, PV(B - 1, J - 1) + 1)
            transpose_rows(0)
            hidden(0, True)
            with pe.Fori(1, E) as e:
                transpose_rows(e)
                expert_out(e - 1)
                hidden(e, False)
                pe.wait_ge(y_copied, CT * e)

            def transpose_xr(n, k, first):
                pe.wait_ge(xr_ok, n + 1)
                if not (first and k < 2):
                    pe.wait_ge(g_t_lo, n - 1)
                for c in range(DC):
                    op = nc.tensor.transpose(ps[:, k % 2, c * P:(c + 1) * P], xr[:, k % 2, c * P:(c + 1) * P], ident[:])
                op.then_inc(g_t_done, 1)

            def gate_product(n, k, first):
                pe.wait_ge(g_t_lo, n + 1)
                if first and k < 2:
                    pe.wait_ge(y_copied, CT * (E - 1) + k + 1)
                else:
                    pe.wait_ge(gate_ok, n - 1)
                for c in range(DC):
                    op = mm3(ps[:, 6 + k % 2, :], xrT_hi[:, k % 2, c * P:(c + 1) * P], xrT_lo[:, k % 2, c * P:(c + 1) * P],
                             wrT_hi[:, c, :], wrT_lo[:, c, :], c == 0, c == DC - 1)
                op.then_inc(g_done, 1)

            transpose_xr(0, 0, True)
            expert_out(E - 1)
            for k in range(1, 4):
                transpose_xr(k, k, True)
                gate_product(k - 1, k - 1, True)
            with pe.Fori(1, NT // 4) as q:
                for k in range(4):
                    transpose_xr(4 * q + k, k, False)
                    gate_product(4 * q + k - 1, (k - 1) % 4, False)
            gate_product(NT - 1, 3, False)


_INS = {"x": "x", "cond": "cond_1024", "tok": "itok_BxS_2_50255", "Wq2": "L0_cond_Wq2", "bq2": "L0_cond_bq2",
        "Wk2": "L0_cond_Wk2", "Wv": "L0_cond_Wv", "bv": "L0_cond_bv", "alpha": "L0_cond_alpha",
        "mk": "L1_cond_time_maa_k", "mr": "L1_cond_time_maa_r", "w_recept": "L1_cond_w_recept",
        "w_key": "L1_cond_w_key", "w_value": "L1_cond_w_value"}


def kernel(**inputs):
    import numpy as _np
    import concourse.bacc as _bacc
    from concourse import mybir as _mybir
    from concourse.bass_utils import run_bass_kernel_spmd as _run

    nc = _bacc.Bacc("TRN2", target_bir_lowering=False, num_devices=1, dynamic_dma_scratch_size=4096)
    arrays, args = {}, {}
    for short, name in _INS.items():
        a = _np.ascontiguousarray(inputs[name])
        arrays[f"in_{name}"] = a
        args[short] = nc.dram_tensor(f"in_{name}", a.shape, _mybir.dt.from_np(a.dtype), kind="ExternalInput").ap()
    args["out"] = nc.dram_tensor("out_0", inputs["x"].shape, _mybir.dt.float32, kind="ExternalOutput").ap()
    build(nc, args)
    r = _run(nc, [arrays], core_ids=[0])
    return r.results[0]["out_0"]
```

```python
from contextlib import ExitStack

import concourse.bass as bass
from concourse import mybir

F32 = mybir.dt.float32
F32R = mybir.dt.float32r
I32 = mybir.dt.int32
U32 = mybir.dt.uint32
ACT = mybir.ActivationFunctionType
ALU = mybir.AluOpType
AX = mybir.AxisListType

P = 128
HASH_PRIME = 5099
MIN_CAPACITY = 4


def build(nc, A):
    B, S, D = A["x"].shape
    E, _, F = A["w_key"].shape
    N = B * S
    CAP = max(MIN_CAPACITY, N // E)
    DC = D // P
    J = S // P
    JH = J // 2
    SH = S // 2
    FC = F // P
    CT = CAP // P
    NT = B * J
    SCALE = 1.0 / float(D) ** 0.5
    RAW = 4
    UNITS = 8
    KU = UNITS // 2
    RES = 4
    assert (D, J, FC, CT, E) == (512, 8, 8, 2, 16)

    xk_dram = nc.dram_tensor("xk_slots", (2 * N, D), F32, kind="Internal").ap()
    y_dram = nc.dram_tensor("y_slots", (N + 1, D), F32, kind="Internal").ap()
    shift_dram = nc.dram_tensor("shifted", (B, P + 1, D), F32, kind="Internal").ap()
    crow_dram = nc.dram_tensor("cond_rows", (B, D), F32, kind="Internal").ap()
    x_v = A["x"].rearrange("b (p j) d -> b p (j d)", p=P)
    out_v = A["out"].rearrange("b (p j) d -> b p (j d)", p=P)
    wkey_v = A["w_key"].rearrange("e (c p) f -> e p c f", p=P)
    wval_v = A["w_value"].rearrange("e (k p) d -> e p k d", p=P)

    with ExitStack() as ctx:
        def sem(name):
            return ctx.enter_context(nc.semaphore(name))

        def alloc(stack):
            return lambda name, shape, dt: stack.enter_context(nc.sbuf_tensor(name, shape, dt))

        sb = alloc(ctx)
        ident = sb("ident", [P, P], F32)
        mean_w = sb("mean_w", [P, P], F32)
        mk_row = sb("mk_row", [P, D], F32)
        mr_row = sb("mr_row", [P, D], F32)
        scat_idx = sb("scat_idx", [P, NT], I32)
        gath_idx = sb("gath_idx", [P, NT], I32)
        idx_now = sb("idx_now", [P, J], I32)
        dx = sb("dx", [P, D], F32)
        with ExitStack() as room:
            row_t = alloc(room)("row_t", [P, CT, D], F32)
        xk = sb("xk", [P, 2, D], F32)
        b_row = sb("b_row", [P, D], F32)
        x_before = sb("x_before", [P, D], F32)
        alpha = sb("alpha", [P, 1], F32)
        u_col = sb("u_col", [P, DC, 2], F32)
        neg_max = sb("neg_max", [P, J], F32)
        row_sum = sb("row_sum", [P, J], F32)
        row_inv = sb("row_inv", [P, J], F32)

        with ExitStack() as room:
            sbs = alloc(room)
            wq_raw = sbs("wq_raw", [P, DC, D], F32)
            wk_raw = sbs("wk_raw", [P, DC, D], F32)
            wv2_raw = sbs("wv2_raw", [P, DC, D], F32)
            wqT_hi = sbs("wqT_hi", [P, DC, D], F32R)
            wqT_lo = sbs("wqT_lo", [P, DC, D], F32R)
            wkT_hi = sbs("wkT_hi", [P, DC, D], F32R)
            wkT_lo = sbs("wkT_lo", [P, DC, D], F32R)
            tok = sbs("tok", [P, NT], I32)
            e_int = sbs("e_int", [P, NT], I32)
            e_f = sbs("e_f", [P, NT], F32)
            own_i = sbs("own_i", [P, NT], I32)
            own_f = sbs("own_f", [P, NT], F32)
            onehot = sbs("onehot", [P, B, J, E], F32)
            rank = sbs("rank", [P, B, J, E], F32)
            tot = sbs("tot", [P, B, E], F32)
            earlier = sbs("earlier", [P, B, E], F32)
            pos = sbs("pos", [P, NT], F32)
            keep = sbs("keep", [P, NT], F32)
            slot = sbs("slot", [P, NT], F32)
            diff = sbs("diff", [P, NT], F32)
        x1 = sb("x1", [P, NT * D], F32)

        with ExitStack() as room:
            sba = alloc(room)
            x_in = sba("x_in", [P, JH, D], F32)
            m_hi = sba("m_hi", [P, DC, D], F32R)
            m_lo = sba("m_lo", [P, DC, D], F32R)
            wv_hi = sba("wv_hi", [P, DC, D], F32R)
            wv_lo = sba("wv_lo", [P, DC, D], F32R)
            xT_hi = sba("xT_hi", [P, DC, S], F32R)
            xT_lo = sba("xT_lo", [P, DC, S], F32R)
            z_hi = sba("z_hi", [P, DC, SH], F32R)
            z_lo = sba("z_lo", [P, DC, SH], F32R)
            prob = sba("prob", [P, S], F32)
            prob_t = sba("prob_t", [P, S], F32)
            pT_hi = sba("pT_hi", [P, J, P], F32R)
            pT_lo = sba("pT_lo", [P, J, P], F32R)
            with ExitStack() as inner:
                sbs = alloc(inner)
                wv1_raw = sbs("wv1_raw", [P, DC, D], F32)
                upper = sbs("upper", [P, P], F32)
                ones = sbs("ones", [P, P], F32)
                cond4 = sbs("cond4", [B, D], F32)
                bq4 = sbs("bq4", [DC, P], F32)
                condT = sbs("condT", [P, DC, B], F32)
                bq_hi = sbs("bq_hi", [P, DC, 2], F32R)
                bq_lo = sbs("bq_lo", [P, DC, 2], F32R)
                bv4 = sbs("bv4", [B, D], F32)
                crow4 = sbs("crow4", [B, D], F32)
                rest = sbs("rest", [P, 1], F32)
            v_hi = sba("v_hi", [P, J, D], F32R)
            v_lo = sba("v_lo", [P, J, D], F32R)

        with ExitStack() as room:
            alloc(room)("below", [P, (RAW + 2 * UNITS) * 2 * D - 2 * D], F32)
            xr_early = alloc(room)("xr_early", [P, 2, D], F32)

        with ExitStack() as room:
            sbm = alloc(room)
            w_raw = sbm("w_raw", [P, RAW, 2 * D], F32)
            wu_hi = sbm("wu_hi", [P, UNITS, 2 * D], F32R)
            wu_lo = sbm("wu_lo", [P, UNITS, 2 * D], F32R)
            with ExitStack() as inner:
                sbf = alloc(inner)
                xrT_hi = sbf("xrT_hi", [P, 2, D], F32R)
                xrT_lo = sbf("xrT_lo", [P, 2, D], F32R)
            with ExitStack() as inner:
                wr_raw = alloc(inner)("wr_raw", [P, DC, D], F32)
            xe_hi = sbm("xe_hi", [P, DC, CAP], F32R)
            xe_lo = sbm("xe_lo", [P, DC, CAP], F32R)
            h_hi = sbm("h_hi", [P, FC, CAP], F32R)
            h_lo = sbm("h_lo", [P, FC, CAP], F32R)
            xrow = sbm("xrow", [P, CT, D], F32)
            with ExitStack() as inner:
                xr = alloc(inner)("xr", [P, 2, D], F32)
            relu = sbm("relu", [P, 2, CAP], F32)
            hsq = sbm("hsq", [P, 2, CAP], F32)
            y_out = sbm("y_out", [P, CT, D], F32)
            wrT_hi = sbm("wrT_hi", [P, DC, D], F32R)
            wrT_lo = sbm("wrT_lo", [P, DC, D], F32R)
            gate_early = sbm("gate_early", [P, 3, D], F32)

        with ExitStack() as room:
            sbf = alloc(room)
            y_got = sbf("y_got", [P, J, D], F32)
            res = sbf("res", [P, RES, D], F32)
            gate = sbf("gate", [P, J, D], F32)

        ps = ctx.enter_context(nc.psum_tensor("ps", [P, 8, 512], F32))
        score_ps = ps[:, 0:2, :].rearrange("p a n -> p (a n)")
        row_ps = ps[:, 5, :]
        misc_ps = ps[:, 2, :]
        counts_ps = ps[:, 3, 0:B * E]

        def tr_bank(n):
            return ps[:, 2 + n % 3 if n < TR0 else (0, 1, 4, 5)[(n - TR0) % 4], :]

        def p_bank(g):
            return ps[:, 2 + g, :]

        def out_bank(n):
            return ps[:, 6 + n % 2, :]

        ld_wq, ld_wk, ld_x, ld_wv2, ld_wv1 = (sem(n) for n in ("ld_wq", "ld_wk", "ld_x", "ld_wv2", "ld_wv1"))
        ld_tok, ld_small, ld_x1, ld_brow, ld_wr, ld_before = (
            sem(n) for n in ("ld_tok", "ld_small", "ld_x1", "ld_brow", "ld_wr", "ld_before"))
        ld_raw = [sem(f"ld_raw{i}") for i in range(RAW)]
        ld_xrow = sem("ld_xrow")
        consts_ok, own_ok, tot_ok, earlier_done, index_ok = (
            sem(n) for n in ("consts_ok", "own_ok", "tot_ok", "earlier_done", "index_ok"))
        misc_done, misc_ok = sem("misc_done"), sem("misc_ok")
        mean_ok, wv_hi_ok, wv_lo_ok, crow_ok, crow_stored = (
            sem(n) for n in ("mean_ok", "wv_hi_ok", "wv_lo_ok", "crow_ok", "crow_stored"))
        zeroed, zero_row, cond_rows = sem("zeroed"), sem("zero_row"), sem("cond_rows")
        tr_done, tr_hi, tr_lo = sem("tr_done"), sem("tr_hi"), sem("tr_lo")
        p_blocks, p_act, p_dve, p_hi, p_lo = (sem(n) for n in ("p_blocks", "p_act", "p_dve", "p_hi", "p_lo"))
        out_done, out_hi, out_free = sem("out_done"), sem("out_hi"), sem("out_free")
        s_done, max_done, exp_done = sem("s_done"), sem("max_done"), sem("exp_done")
        row_done, row_ok, x1_ok = sem("row_done"), sem("row_ok"), sem("x1_ok")
        shift_out, shift_in = sem("shift_out"), sem("shift_in")
        scattered = [sem(f"scattered{i}") for i in range(2)]
        t_done, t_hi, t_lo = sem("t_done"), sem("t_hi"), sem("t_lo")
        r_blocks, r_act, r_dve = sem("r_blocks"), sem("r_act"), sem("r_dve")
        v_used, w_hi, w_lo = sem("v_used"), sem("w_hi"), sem("w_lo")
        h_done, relu_ok, h_hi_ok, h_lo_ok = sem("h_done"), sem("relu_ok"), sem("h_hi_ok"), sem("h_lo_ok")
        y_done, y_copied = sem("y_done"), sem("y_copied")
        y_stored = [sem(f"y_stored{i}") for i in range(CT)]
        xr_ok, g_t_done, g_t_hi, g_t_lo = sem("xr_ok"), sem("g_t_done"), sem("g_t_hi"), sem("g_t_lo")
        g_done, gate_ok, res_ok = sem("g_done"), sem("gate_ok"), sem("res_ok")
        y_here = [sem(f"y_here{i}") for i in range(J)]
        stored = [sem(f"stored{i}") for i in range(RES)]
        settled = sem("settled")
        dve_chain, pool_chain = sem("dve_chain"), sem("pool_chain")
        inv_ok, xr_sub, xr_mul = sem("inv_ok"), sem("xr_sub"), sem("xr_mul")
        vsum_step, xk_step, idx_copied, hsq_ok, scaled, scaled_pool = (
            sem(n) for n in ("vsum_step", "xk_step", "idx_copied", "hsq_ok", "scaled", "scaled_pool"))

        TR0, OUT0, HI0 = 8, 6, 4

        def TR(b, k):
            return TR0 + 2 * DC * b + k

        def OUT(b, k):
            return OUT0 + 24 * b + k

        def PV(b, i):
            return OUT(b, 12 + i if i < 3 else 16 + i)

        def HI(b, k):
            return HI0 + 16 * b + k

        def W(e, u):
            return UNITS * e + u

        def MT(e, g):
            return DC + 2 * e + g

        def half(p):
            return 1 - p

        def query(i):
            return (i + JH) % J

        POOL_SCALES = (3, 7)

        def block_move(a, c):
            return (ps[32 * c:32 * c + 32, 2:4, :].rearrange("p g (k a n) -> p (g k) a n", a=4, n=32)[:, :, a, :],
                    prob_t[32 * a:32 * a + 32, :].rearrange("p (k c n) -> p k c n", c=4, n=32)[:, :, c, :])

        def row_move(a, c):
            return (ps[32 * c:32 * c + 32, 0:2, :].rearrange("p g (k t a n) -> p (g k) t a n", t=CT, a=4, n=32)
                    [:, :, :, a, :],
                    row_t[32 * a:32 * a + 32, :, :].rearrange("p t (k c n) -> p k t c n", c=4, n=32)[:, :, :, c, :])

        EARLY = 3

        def gate_tile(b, k):
            return k if not isinstance(b, int) or b else (1, 2, 3, 0, 4, 5, 6, 7)[k]

        def pool_scales(k):
            return k in POOL_SCALES

        def scaled_at(b, k):
            mine = [i for i in range(J) if pool_scales(i) == pool_scales(k)]
            return len(mine) * b + mine.index(k) + 1

        def gate_at(b, k):
            return gate_early[:, k, :] if isinstance(b, int) and b == 0 and k < EARLY else gate[:, k, :]

        def tile(b, j):
            return x1[:, bass.ds((b * J + j) * D, D)]

        def batch_of(view, b):
            return view[b] if isinstance(b, int) else view[bass.ds(b, 1)].rearrange("a p n -> (a p) n")

        block = ctx.enter_context(nc.Block())

        @block.sync
        def _(sp):
            x_in_flat = x_in[:].rearrange("p j d -> p (j d)")
            sp.dma_start(wq_raw[:], A["Wq2"].rearrange("(c p) e -> p c e", p=P)).then_inc(ld_wq, 16)
            sp.dma_start(wk_raw[:], A["Wk2"].rearrange("(c p) e -> p c e", p=P)).then_inc(ld_wk, 16)
            sp.dma_start(x_in_flat, x_v[0][:, half(0) * JH * D:(half(0) + 1) * JH * D]).then_inc(ld_x, 16)
            sp.dma_start(wv1_raw[:], A["Wv"][0:D, :].rearrange("(c p) e -> p c e", p=P)).then_inc(ld_wv1, 16)

            def load_half(b, p, after):
                h = half(p)
                sp.wait_ge(tr_done, after + 1)
                sp.dma_start(x_in_flat, batch_of(x_v, b)[:, h * JH * D:(h + 1) * JH * D]).then_inc(ld_x, 16)

            def load_residual(b):
                sp.dma_start(x1[:, bass.ds(b * J * D, J * D)], batch_of(x_v, b)).then_inc(ld_x1, 16)

            def load_row(b):
                sp.dma_start(b_row[:], crow_dram[bass.ds(b, 1), :].partition_broadcast(P)).then_inc(ld_brow, 16)

            load_half(0, 1, TR(0, 3))
            sp.dma_start(wv2_raw[:], A["Wv"][D:2 * D, :].rearrange("(c p) e -> p c e", p=P)).then_inc(ld_wv2, 16)
            sp.wait_ge(crow_ok, 1)
            sp.dma_start(crow_dram, crow4[:]).then_inc(crow_stored, 16)
            load_half(1, 0, TR(0, 7))
            sp.wait_ge(wv_lo_ok, 1)
            load_residual(0)
            sp.wait_ge(crow_stored, 16)
            load_row(0)
            sp.wait_ge(consts_ok, 1)
            sp.dma_start(xk_dram[0:N, :].rearrange("(p r) d -> p r d", p=P),
                         dx[:].unsqueeze(1).broadcast_to((P, N // P, D))).then_inc(zeroed, 16)

            def batch_loads(b, last):
                load_half(b, 1, TR(b, 3))
                if not last:
                    load_half(b + 1, 0, TR(b, 7))
                sp.wait_ge(ld_x1, 16 * b)
                if last:
                    sp.wait_ge(index_ok, 1)
                load_residual(b)
                sp.wait_ge(x1_ok, J * b)
                load_row(b)

            with sp.Fori(1, B - 1) as b:
                batch_loads(b, False)
            batch_loads(B - 1, True)

            def load_unit(e, u):
                if u < KU:
                    src = wkey_v[bass.ds(e, 1), :, :, u * CAP:(u + 1) * CAP].rearrange("a p c f -> (a p) c f")
                    dst = w_raw[:, u % RAW, :].rearrange("p (c f) -> p c f", c=DC)
                else:
                    v = 2 * (u - KU)
                    src = wval_v[bass.ds(e, 1), :, v:v + 2, :].rearrange("a p k d -> (a p) k d")
                    dst = w_raw[:, u % RAW, :].rearrange("p (k d) -> p k d", k=2)
                sp.dma_start(dst, src).then_inc(ld_raw[u % RAW], 16)

            def load_rows(e):
                sp.dma_start(xrow[:], xk_dram[bass.ds(e * CAP, CAP), :].rearrange("(t p) d -> p t d", p=P)
                             ).then_inc(ld_xrow, 16)

            sp.wait_ge(out_done, OUT(B - 1, 18) + 1)
            for u in range(RAW):
                load_unit(0, u)
            sp.wait_ge(s_done, B * J)
            sp.dma_start(wr_raw[:], A["w_recept"].rearrange("(c p) d -> p c d", p=P)).then_inc(ld_wr, 16)
            for q in scattered:
                sp.wait_ge(q, 16 * NT // 2)
            load_rows(0)

            def load_before(b):
                sp.dma_start(x_before[:], batch_of(shift_dram[:, 0:P, :], b)).then_inc(ld_before, 16)

            load_before(0)

            def expert_loads(e, first, last):
                if not last:
                    sp.wait_ge(*((t_done, MT(0, 1) + 1) if first else (r_blocks, e)))
                    load_rows(e + 1)
                for u in range(RAW if first else 0, UNITS):
                    sp.wait_ge(w_lo, W(e, u) - RAW + 1)
                    load_unit(e, u)

            expert_loads(0, True, False)
            with sp.Fori(1, E - 1) as e:
                expert_loads(e, False, False)
            expert_loads(E - 1, False, True)

            def batch_results(b, ahead):
                for k in range(J):
                    j = gate_tile(b, k)
                    sp.wait_ge(res_ok, b * J + k + 1)
                    sp.dma_start(batch_of(out_v, b)[:, j * D:(j + 1) * D], res[:, k % RES, :]
                                 ).then_inc(stored[k % RES], 16)
                    if k == JH and ahead:
                        sp.wait_ge(xr_ok, (b + 1) * J + 1)
                        load_before(b + 2)

            sp.wait_ge(xr_ok, EARLY + 1)
            load_before(1)
            batch_results(0, True)
            with sp.Fori(1, B - 2) as b:
                batch_results(b, True)
            for b in range(B - 2, B):
                batch_results(b, False)
            for q in stored:
                sp.wait_ge(q, 16 * NT // RES)

        @block.scalar
        def _(act):
            def hi(out, in_, done, bias=0.0, scale=1.0, func=ACT.Copy):
                nc.scalar.activation(out, in_, func, bias=bias, scale=scale).then_inc(done, 1)

            def tr_split(n, out):
                act.wait_ge(tr_done, n + 1)
                hi(out, tr_bank(n), tr_hi)

            act.dma_start(tok[:].rearrange("p (b j) -> p b j", b=B),
                          A["tok"].rearrange("b (p j) -> p b j", p=P)).then_inc(ld_tok, 16)
            for dst, src in ((bq4[:], A["bq2"].rearrange("(c p) -> c p", p=P)),
                             (cond4[:], A["cond"]),
                             (bv4[:], A["bv"].rearrange("(a d) -> a d", a=1).partition_broadcast(B)),
                             (alpha[:], A["alpha"].rearrange("(a d) -> a d", a=1).partition_broadcast(P)),
                             (mk_row[:], A["mk"].rearrange("(a d) -> a d", a=1).partition_broadcast(P)),
                             (mr_row[:], A["mr"].rearrange("(a d) -> a d", a=1).partition_broadcast(P))):
                act.dma_start(dst, src).then_inc(ld_small, 16)
            for k in range(2 * DC):
                tr_split(k, (wqT_hi, wkT_hi)[k // DC][:, k % DC, :])
            def x_split(b, p):
                h = half(p)
                for c in range(DC):
                    act.wait_ge(tr_done, TR(b, DC * p + c) + 1)
                    hi(xT_hi[:, c, h * SH:(h + 1) * SH], tr_bank(TR0 + DC * p + c), tr_hi)

            x_split(0, 0)
            act.wait_ge(misc_done, 1)
            for k in range(2):
                op = nc.scalar.activation(bq_hi[:, :, k], misc_ps[:, 0:DC], ACT.Copy)
            op.then_inc(misc_ok, 1)
            for k in range(DC):
                act.wait_ge(out_done, k + 1)
                hi(m_hi[:, k, :], out_bank(k), out_hi, scale=SCALE)

            def z_split(b, k0):
                for c in range(DC):
                    act.wait_ge(out_done, OUT(b, k0 + c) + 1)
                    hi(z_hi[:, c, :], out_bank(OUT0 + k0 + c), out_hi, bias=u_col[:, c, 0:1], func=ACT.Identity)

            def p_move(j):
                out, in_ = block_move(j % 4, j // 4)
                op = nc.scalar.activation(out, in_, ACT.Copy)
                if j == J - 1:
                    op.then_inc(p_act, 1)

            def batch(b, first):
                if not first:
                    x_split(b, 0)
                x_split(b, 1)
                if first:
                    act.wait_ge(crow_ok, 1)
                z_split(b, 0)
                if first:
                    act.wait_ge(ld_wv2, 16)
                    nc.scalar.activation(wv_hi[:].rearrange("p c n -> p (c n)"),
                                         wv2_raw[:].rearrange("p c n -> p (c n)"), ACT.Copy).then_inc(wv_hi_ok, 1)
                for i in range(J):
                    act.wait_ge(max_done, b * J + i + 1)
                    nc.scalar.activation(prob[:], score_ps, ACT.Exp, bias=neg_max[:, i:i + 1],
                                         accum_out=row_sum[:, i:i + 1]).then_inc(exp_done, 1)
                    if not (first and i == 0):
                        act.wait_ge(p_lo, 2 * (b * J + i))
                    act.wait_ge(p_blocks, b * J + i + 1)
                    if i == 0:
                        for j in range(J):
                            p_move(j)
                            act.wait_ge(out_done, OUT(b, DC + j) + 1)
                            if j == 0:
                                act.wait_ge(vsum_step, (2 * J - 1) * b)
                                if first:
                                    act.wait_ge(crow_stored, 16)
                            hi(v_hi[:, j, :], out_bank(OUT0 + DC + j), out_hi)
                    else:
                        for j in range(J):
                            p_move(j)
                        act.wait_ge(out_done, PV(b, i - 1) + 1)
                    act.wait_ge(p_act, b * J + i + 1)
                    act.wait_ge(p_dve, b * J + i + 1)
                    for g in range(2):
                        hi(pT_hi[:, JH * g:JH * (g + 1), :].rearrange("p a n -> p (a n)"), p_bank(g), p_hi)
                    if i == JH - 1:
                        z_split(b, 15)

            batch(0, True)
            with act.Fori(1, B) as b:
                batch(b, False)

            def unit_split(e, u, first):
                act.wait_ge(ld_raw[u % RAW], 16 * (2 * e + u // RAW + 1))
                if first:
                    act.wait_ge(s_done, B * J)
                else:
                    if u < KU:
                        act.wait_ge(h_done, FC * (e - 1) + 2 * u + 2)
                    elif u < UNITS - 1:
                        act.wait_ge(v_used, (KU - 1) * (e - 1) + u - KU + 1)
                    else:
                        act.wait_ge(y_done, CT * e)
                hi(wu_hi[:, u, :], w_raw[:, u % RAW, :], w_hi)

            def row_moves(e):
                act.wait_ge(r_blocks, e)
                act.wait_ge(t_lo, MT(e, 0))
                for a in range(4):
                    op = nc.scalar.activation(*row_move(a, 3), ACT.Copy)
                op.then_inc(r_act, 1)

            def rows_split(e, first):
                if not first:
                    act.wait_ge(r_act, e)
                    act.wait_ge(r_dve, e)
                for g in range(2):
                    if first:
                        act.wait_ge(t_done, MT(e, g) + 1)
                    hi(xe_hi[:, 2 * g:2 * g + 2, :].rearrange("p a n -> p (a n)"), ps[:, g, :], t_hi)

            def copy_y_half(e, t):
                act.wait_ge(y_done, CT * e + t + 1)
                act.wait_ge(y_stored[t], 16 * e)
                nc.scalar.activation(y_out[:, t, :], ps[:, 6 + t, :], ACT.Copy).then_inc(y_copied, 1)

            def copy_y(e):
                for t in range(CT):
                    copy_y_half(e, t)

            def hidden(e, first):
                for f in range(FC):
                    act.wait_ge(h_done, FC * e + f + 1)
                    if not (first and f < 2):
                        act.wait_ge(h_lo_ok, FC * e + f - 1)
                    nc.scalar.activation(relu[:, f % 2, :], ps[:, 2 + f % 4, 0:CAP], ACT.Relu).then_inc(relu_ok, 1)
                    act.wait_ge(relu_ok, FC * e + f + 1)
                    nc.scalar.activation(h_hi[:, f, :], relu[:, f % 2, :], ACT.Square).then_inc(h_hi_ok, 1)
                    if f % 2:
                        unit_split(e, KU + f // 2, first)

            def gate_split(n, k, first):
                act.wait_ge(g_t_done, n + 1)
                if not (first and k < 2):
                    act.wait_ge(g_done, n - 1)
                hi(xrT_hi[:, k % 2, :], ps[:, k % 2, :], g_t_hi)

            def sigmoid(b, k, first):
                n = b * J + k
                act.wait_ge(g_done, n + 1)
                if not first:
                    act.wait_ge(scaled_pool if pool_scales(k) else scaled, scaled_at(b - 1, k))
                nc.scalar.activation(gate_at(b, k), ps[:, 6 + k % 2, :], ACT.Sigmoid).then_inc(gate_ok, 1)

            for u in range(KU):
                unit_split(0, u, True)
            act.wait_ge(vsum_step, (2 * J - 1) * B)
            for g in range(DC):
                act.wait_ge(t_done, g + 1)
                hi(wrT_hi[:, g, :], ps[:, g % 2, :], t_hi)
            gate_split(0, 0, True)
            for k in range(1, EARLY):
                gate_split(k, k, True)
                sigmoid(0, k - 1, True)
            sigmoid(0, EARLY - 1, True)
            rows_split(0, True)
            row_moves(1)
            hidden(0, True)

            def expert(e, last):
                rows_split(e, False)
                for u in range(KU):
                    unit_split(e, u, False)
                copy_y(e - 1)
                if not last:
                    row_moves(e + 1)
                hidden(e, False)

            with act.Fori(1, E - 1) as e:
                expert(e, False)
            expert(E - 1, True)

            copy_y_half(E - 1, 0)
            gate_split(EARLY, EARLY, True)
            copy_y_half(E - 1, 1)
            for k in range(EARLY + 1, J):
                gate_split(k, k, True)
                sigmoid(0, k - 1, True)

            def gates(b, first):
                for k in range(J):
                    gate_split(b * J + k, k, False)
                    if k:
                        sigmoid(b, k - 1, False)
                    else:
                        sigmoid(b - 1, J - 1, first)

            gates(1, True)
            with act.Fori(2, B) as b:
                gates(b, False)
            sigmoid(B - 1, J - 1, False)

        @block.vector
        def _(dve):
            chain = [0]

            def link(op):
                chain[0] += 1
                op.then_inc(dve_chain, 1)
                dve.wait_ge(dve_chain, chain[0])

            tt, ts, stt = nc.vector.tensor_tensor, nc.vector.tensor_scalar, nc.vector.scalar_tensor_tensor

            def lo(out, in_, hi_part, done):
                tt(out, in_, hi_part.bitcast(F32), ALU.subtract).then_inc(done, 1)

            for k in range(2 * DC):
                dve.wait_ge(tr_hi, k + 1)
                lo((wqT_lo, wkT_lo)[k // DC][:, k % DC, :], tr_bank(k), (wqT_hi, wkT_hi)[k // DC][:, k % DC, :], tr_lo)

            def x_split(b, p):
                h = half(p)
                for c in range(DC):
                    dve.wait_ge(tr_hi, TR(b, DC * p + c) + 1)
                    lo(xT_lo[:, c, h * SH:(h + 1) * SH], tr_bank(TR0 + DC * p + c),
                       xT_hi[:, c, h * SH:(h + 1) * SH], tr_lo)

            x_split(0, 0)
            dve.wait_ge(misc_ok, 1)
            for k in range(2):
                tt(bq_lo[:, :, k], misc_ps[:, 0:DC], bq_hi[:, :, k].bitcast(F32), ALU.subtract)
            nc.vector.tensor_copy(condT[:].rearrange("p c b -> p (c b)"), misc_ps[:, DC:DC + DC * B]
                                  ).then_inc(misc_ok, 1)
            dve.wait_ge(ld_small, 16 * 6)
            dve.wait_ge(consts_ok, 1)
            link(ts(rest[:], alpha[:], -1.0, 1.0, ALU.mult, ALU.add))
            ts(mean_w[:], mean_w[:], alpha[:], None, ALU.mult).then_inc(mean_ok, 1)
            dve.wait_ge(ld_tok, 16)
            link(ts(e_int[:], tok[:], E - 1, None, ALU.bitwise_and))
            link(ts(tok[:], e_int[:], float(HASH_PRIME % E), None, ALU.mult))
            link(ts(e_int[:], tok[:], E - 1, None, ALU.bitwise_and))
            link(nc.vector.tensor_copy(e_f[:], e_int[:]))
            oh = onehot[:].rearrange("p b j e -> p (b j) e")
            for e in range(E):
                op = ts(oh[:, :, e], e_f[:], float(e), None, ALU.is_equal)
            link(op)
            link(nc.vector.tensor_reduce(tot[:], onehot[:].rearrange("p b j e -> p b e j"), AX.X, ALU.add))
            link(nc.vector.memset(earlier[:], 0.0))
            for b in range(1, B - 1):
                link(tt(earlier[:, b, :], earlier[:, b - 1, :], tot[:, b - 1, :], ALU.add))
            tt(earlier[:, B - 1, :], earlier[:, B - 2, :], tot[:, B - 2, :], ALU.add).then_inc(tot_ok, 1)
            for k in range(DC):
                dve.wait_ge(out_hi, k + 1)
                stt(m_lo[:, k, :], out_bank(k), SCALE, m_hi[:, k, :].bitcast(F32), ALU.mult, ALU.subtract
                    ).then_inc(out_free, 1)
            dve.wait_ge(out_done, 5)
            ts(u_col[:].rearrange("p c k -> p (c k)"), out_bank(4)[:, 0:2 * DC], SCALE, None, ALU.mult
               ).then_inc(out_free, 1)
            dve.wait_ge(out_done, 6)
            tt(crow4[:], out_bank(5)[0:B, :], bv4[:], ALU.add).then_inc(out_free, 1)
            dve.wait_ge(out_free, 6)
            ts(crow4[:], crow4[:], rest[0:B, :], None, ALU.mult).then_inc(crow_ok, 1)

            dve.wait_ge(earlier_done, 1)
            link(nc.vector.tensor_copy(rank[:, :, 0, :], counts_ps.rearrange("p (b e) -> p b e", b=B)))

            def token_slots():
                for j in range(1, J):
                    link(tt(rank[:, :, j, :], rank[:, :, j - 1, :], onehot[:, :, j - 1, :], ALU.add))
                rank_f = rank[:].rearrange("p b j e -> p (b j e)")
                link(tt(rank_f, rank_f, onehot[:].rearrange("p b j e -> p (b j e)"), ALU.mult))
                link(nc.vector.tensor_reduce(pos[:], rank[:].rearrange("p b j e -> p (b j) e"), AX.X, ALU.add))
                link(ts(keep[:], pos[:], float(CAP), None, ALU.is_lt))
                link(stt(slot[:], e_f[:], float(CAP), pos[:], ALU.mult, ALU.add))
                dve.wait_ge(own_ok, 1)
                link(nc.vector.tensor_copy(own_f[:], own_i[:]))
                link(tt(diff[:], slot[:], own_f[:], ALU.subtract))
                link(tt(diff[:], diff[:], keep[:], ALU.mult))
                link(tt(scat_idx[:], diff[:], own_f[:], ALU.add))
                link(ts(diff[:], slot[:], float(-N), None, ALU.add))
                link(tt(diff[:], diff[:], keep[:], ALU.mult))
                ts(gath_idx[:], diff[:], float(N), None, ALU.add).then_inc(index_ok, 1)

            def pv_evacuate(b, i):
                dve.wait_ge(out_done, PV(b, i) + 1)
                dve.wait_ge(ld_x1, 16 * (b + 1))
                dve.wait_ge(inv_ok, b * J + i + 1)
                row = tile(b, query(i))
                stt(row, out_bank(PV(0, i)), row_inv[:, i:i + 1], row, ALU.mult, ALU.add
                    ).then_inc(out_free, 1)

            def z_split(b, k0, h0):
                for c in range(DC):
                    dve.wait_ge(out_hi, HI(b, h0 + c) + 1)
                    stt(z_lo[:, c, :], out_bank(OUT0 + k0 + c), u_col[:, c, 0:1], z_hi[:, c, :].bitcast(F32),
                        ALU.add, ALU.subtract).then_inc(out_free, 1)

            def p_move(j):
                op = nc.vector.tensor_copy(*block_move(j % 4, 2 + j // 4))
                if j == J - 1:
                    op.then_inc(p_dve, 1)

            def batch(b, first):
                if not first:
                    x_split(b, 0)
                    pv_evacuate(b - 1, J - 1)
                x_split(b, 1)
                z_split(b, 0, 0)
                if first:
                    dve.wait_ge(wv_hi_ok, 1)
                    lo(wv_lo[:].rearrange("p c n -> p (c n)"), wv2_raw[:].rearrange("p c n -> p (c n)"),
                       wv_hi[:].rearrange("p c n -> p (c n)"), wv_lo_ok)
                for i in range(J):
                    dve.wait_ge(s_done, b * J + i + 1)
                    nc.vector.tensor_reduce(neg_max[:, i:i + 1], score_ps, AX.X, ALU.max, negate=True
                                            ).then_inc(max_done, 1)
                    dve.wait_ge(exp_done, b * J + i + 1)
                    if not (first and i == 0):
                        dve.wait_ge(p_act, b * J + i)
                    nc.vector.transpose(prob_t[:], prob[:]).then_inc(p_blocks, 1)
                    nc.vector.reciprocal(row_inv[:, i:i + 1], row_sum[:, i:i + 1]).then_inc(inv_ok, 1)
                    dve.wait_ge(p_blocks, b * J + i + 1)
                    for j in range(J):
                        p_move(j)
                        if i == 0:
                            dve.wait_ge(out_hi, HI(b, DC + j) + 1)
                            lo(v_lo[:, j, :], out_bank(OUT0 + DC + j), v_hi[:, j, :], out_free)
                    if i:
                        pv_evacuate(b, i - 1)
                    for g in range(2):
                        dve.wait_ge(p_hi, 2 * (b * J + i) + g + 1)
                        lo(pT_lo[:, JH * g:JH * (g + 1), :].rearrange("p a n -> p (a n)"), p_bank(g),
                           pT_hi[:, JH * g:JH * (g + 1), :].rearrange("p a n -> p (a n)"), p_lo)
                    if i == 3:
                        dve.wait_ge(row_done, b + 1)
                        dve.wait_ge(ld_brow, 16 * (b + 1))
                        tt(b_row[:], row_ps, b_row[:], ALU.add).then_inc(row_ok, 1)
                    if first and i == 0:
                        token_slots()
                    if i == JH - 1:
                        z_split(b, 15, 12)

            batch(0, True)
            with dve.Fori(1, B) as b:
                batch(b, False)
            def unit_split(e, u):
                dve.wait_ge(w_hi, W(e, u) + 1)
                lo(wu_lo[:, u, :], w_raw[:, u % RAW, :], wu_hi[:, u, :], w_lo)

            def row_blocks(e, first):
                dve.wait_ge(ld_xrow, 16 * (e + 1))
                if not first:
                    dve.wait_ge(r_act, e - 1)
                nc.vector.transpose(row_t[:].rearrange("p t d -> p (t d)"), xrow[:].rearrange("p t d -> p (t d)")
                                    ).then_inc(r_blocks, 1)
                dve.wait_ge(r_blocks, e)

            def row_moves():
                for c in range(3):
                    for a in range(4):
                        op = nc.vector.tensor_copy(*row_move(a, c))
                op.then_inc(r_dve, 1)

            def rows_split(e):
                for g in range(2):
                    dve.wait_ge(t_hi, MT(e, g) + 1)
                    lo(xe_lo[:, 2 * g:2 * g + 2, :].rearrange("p a n -> p (a n)"), ps[:, g, :],
                       xe_hi[:, 2 * g:2 * g + 2, :].rearrange("p a n -> p (a n)"), t_lo)

            def shifted_rows(b, k, rows):
                n, j = b * J + k, gate_tile(b, k)
                if j == 0:
                    dve.wait_ge(ld_before, 16 * (b + 1))
                before = x_before[:] if j == 0 else tile(b, j - 1)
                row = rows[:, k % 2, :]
                tt(row, before, tile(b, j), ALU.subtract).then_inc(xr_sub, 1)
                dve.wait_ge(xr_sub, n + 1)
                tt(row, row, mr_row[:], ALU.mult).then_inc(xr_mul, 1)
                dve.wait_ge(xr_mul, n + 1)
                tt(row, row, tile(b, j), ALU.add).then_inc(xr_ok, 1)

            def gate_split(n, k):
                dve.wait_ge(g_t_hi, n + 1)
                lo(xrT_lo[:, k % 2, :], ps[:, k % 2, :], xrT_hi[:, k % 2, :], g_t_lo)

            dve.wait_ge(s_done, B * J)
            dve.wait_ge(x1_ok, J)
            shifted_rows(0, 0, xr_early)
            shifted_rows(0, 1, xr_early)
            pv_evacuate(B - 1, J - 1)
            for g in range(DC):
                dve.wait_ge(t_hi, g + 1)
                lo(wrT_lo[:, g, :], ps[:, g % 2, :], wrT_hi[:, g, :], t_lo)
            for k in range(EARLY):
                gate_split(k, k)
                if k + 2 < EARLY:
                    dve.wait_ge(g_t_done, k + 1)
                    shifted_rows(0, k + 2, xr_early)
            unit_split(0, 0)
            rows_split(0)
            for u in range(1, KU):
                unit_split(0, u)
            row_blocks(1, True)
            row_moves()

            def expert(e, last):
                for u in range(KU, UNITS):
                    unit_split(e - 1, u)
                rows_split(e)
                for u in range(KU):
                    unit_split(e, u)
                if not last:
                    row_blocks(e + 1, False)
                    row_moves()

            with dve.Fori(1, E - 1) as e:
                expert(e, False)
            expert(E - 1, True)
            for u in range(KU, UNITS):
                unit_split(E - 1, u)

            def scale_y(b, k):
                j = gate_tile(b, k)
                dve.wait_ge(gate_ok, b * J + k + 1)
                dve.wait_ge(y_here[j], 16 * (b + 1))
                tt(y_got[:, j, :], y_got[:, j, :], gate_at(b, k), ALU.mult).then_inc(scaled, 1)

            dve.wait_ge(h_lo_ok, FC * E)
            dve.wait_ge(x1_ok, NT)
            for k in range(EARLY, J):
                if k >= EARLY + 2:
                    dve.wait_ge(g_t_done, k - 1)
                shifted_rows(0, k, xr)
                if k > EARLY:
                    gate_split(k - 1, k - 1)

            def gate_rows(b, k):
                dve.wait_ge(g_t_done, b * J + k - 1)
                shifted_rows(b, k, xr)
                gate_split(b * J + k - 1, (k - 1) % 2)

            def gates(b):
                for k in range(J):
                    gate_rows(b, k)
                    if not pool_scales(k):
                        scale_y(b - 1, k)

            gates(1)
            with dve.Fori(2, B - 1) as b:
                gates(b)
            todo = [(b, k) for b in (B - 2, B - 1) for k in range(J) if not pool_scales(k)]
            for k in range(J):
                gate_rows(B - 1, k)
                for _ in range(2):
                    if todo[0] <= (B - 1, k - 2):
                        scale_y(*todo.pop(0))
            gate_split(NT - 1, 1)
            for b, k in todo:
                scale_y(b, k)

        @block.gpsimd
        def _(pool):
            chain = [0]

            def link(op):
                chain[0] += 1
                op.then_inc(pool_chain, 1)
                pool.wait_ge(pool_chain, chain[0])

            def settle():
                pool.sem_inc(settled, 1)

            tt = nc.gpsimd.tensor_tensor
            link(nc.gpsimd.memset(ident[:], 0.0))
            link(nc.gpsimd.affine_select(out=ident[:], in_=ident[:], compare_op=ALU.not_equal, fill=1.0, base=0,
                                         pattern=[[-1, P]], channel_multiplier=1))
            link(nc.gpsimd.memset(upper[:], 1.0))
            link(nc.gpsimd.affine_select(out=upper[:], in_=upper[:], compare_op=ALU.is_gt, fill=0.0, base=0,
                                         pattern=[[1, P]], channel_multiplier=-1))
            link(nc.gpsimd.memset(ones[:], 1.0))
            link(nc.gpsimd.memset(dx[:], 0.0))
            nc.gpsimd.memset(mean_w[:], -1.0 / S).then_inc(consts_ok, 1)
            nc.gpsimd.iota(own_i[:].rearrange("p (b j) -> p b j", b=B), [[S, B], [1, J]], base=N,
                           channel_multiplier=J).then_inc(own_ok, 1)
            pool.dma_start(shift_dram[:, 0, :], A["cond"]).then_inc(cond_rows, 16)
            pool.dma_start(y_dram[N:N + 1, :], dx[0:1, :]).then_inc(zero_row, 16)
            pool.wait_ge(zeroed, 16)
            pool.wait_ge(zero_row, 16)
            pool.wait_ge(cond_rows, 16)

            def x1_tile(b, i):
                pool.wait_ge(out_free, PV(b, i) + 1)
                pool.wait_ge(row_ok, b + 1)
                settle()
                row = tile(b, query(i))
                tt(row, row, b_row[:], ALU.add).then_inc(x1_ok, 1)
                pool.wait_ge(x1_ok, b * J + i + 1)

            def xk_tile(b, k, j, before):
                step = 3 * (b * J + k)
                settle()
                tt(dx[:], before, tile(b, j), ALU.subtract).then_inc(xk_step, 1)
                pool.wait_ge(xk_step, step + 1)
                tt(dx[:], dx[:], mk_row[:], ALU.mult).then_inc(xk_step, 1)
                pool.wait_ge(xk_step, step + 2)
                pool.wait_ge(scattered[k % 2], 16 * (b * (J // 2) + k // 2))
                settle()
                tt(xk[:, k % 2, :], dx[:], tile(b, j), ALU.add).then_inc(xk_step, 1)
                pool.wait_ge(xk_step, step + 3)
                settle()
                pool.indirect_dma_start(
                    out=xk_dram, out_offset=bass.IndirectOffsetOnAxis(ap=idx_now[:, j:j + 1].bitcast(U32), axis=0),
                    in_=xk[:, k % 2, :], in_offset=None).then_inc(scattered[k % 2], 16)

            def batch(b, first):
                if first:
                    pool.wait_ge(index_ok, 1)
                for q in scattered:
                    pool.wait_ge(q, 16 * (J // 2) * b)
                settle()
                nc.gpsimd.tensor_copy(idx_now[:], scat_idx[:, bass.ds(b * J, J)]).then_inc(idx_copied, 1)
                steps = 2 * J - 1
                if not first:
                    pool.wait_ge(row_done, b)
                pool.wait_ge(out_free, OUT(b, DC) + 1)
                tt(dx[:], v_hi[:, 0, :].bitcast(F32), v_lo[:, 0, :].bitcast(F32), ALU.add).then_inc(vsum_step, 1)
                for k in range(1, steps):
                    j = (k + 1) // 2
                    if k % 2:
                        pool.wait_ge(out_free, OUT(b, DC + j) + 1)
                    pool.wait_ge(vsum_step, steps * b + k)
                    tt(dx[:], dx[:], (v_hi, v_lo)[(k + 1) % 2][:, j, :].bitcast(F32), ALU.add).then_inc(vsum_step, 1)
                pool.wait_ge(idx_copied, b + 1)
                for i in range(J):
                    j = query(i)
                    x1_tile(b, i)
                    if j == J - 1:
                        settle()
                        pool.dma_start(batch_of(shift_dram[:, 1:P + 1, :], b), tile(b, j)).then_inc(shift_out, 16)
                    if i:
                        if j == 0:
                            pool.wait_ge(shift_in, 16 * (b + 1))
                        xk_tile(b, i - 1, j, tile(b, j - 1) if j else x_before[:])
                    if j == J - 1:
                        pool.wait_ge(shift_out, 16 * (b + 1))
                        settle()
                        pool.dma_start(x_before[:], batch_of(shift_dram[:, 0:P, :], b)).then_inc(shift_in, 16)
                xk_tile(b, J - 1, query(0), tile(b, query(J - 1)))

            batch(0, True)
            with pool.Fori(1, B) as b:
                batch(b, False)

            def hidden(e, first):
                for f in range(FC):
                    n = FC * e + f
                    pool.wait_ge(relu_ok, n + 1)
                    tt(hsq[:, f % 2, :], relu[:, f % 2, :], relu[:, f % 2, :], ALU.mult).then_inc(hsq_ok, 1)
                    pool.wait_ge(hsq_ok, n + 1)
                    pool.wait_ge(h_hi_ok, n + 1)
                    tt(h_lo[:, f, :], hsq[:, f % 2, :], h_hi[:, f, :].bitcast(F32), ALU.subtract
                       ).then_inc(h_lo_ok, 1)

            def store_y(e):
                for t in range(CT):
                    pool.wait_ge(y_copied, CT * e + t + 1)
                    settle()
                    pool.dma_start(y_dram[bass.ds(e * CAP + t * P, P), :], y_out[:, t, :]).then_inc(y_stored[t], 16)

            hidden(0, True)
            with pool.Fori(1, E) as e:
                store_y(e - 1)
                hidden(e, False)
            store_y(E - 1)

            def indices(b):
                settle()
                nc.gpsimd.tensor_copy(idx_now[:], gath_idx[:, bass.ds(b * J, J)]).then_inc(idx_copied, 1)
                pool.wait_ge(idx_copied, B + b + 1)
                settle()

            def gather(j):
                pool.indirect_dma_start(
                    out=y_got[:, j, :], out_offset=None, in_=y_dram,
                    in_offset=bass.IndirectOffsetOnAxis(ap=idx_now[:, j:j + 1].bitcast(U32), axis=0)
                ).then_inc(y_here[j], 16)

            for q in scattered:
                pool.wait_ge(q, 16 * NT // 2)
            for q in y_stored:
                pool.wait_ge(q, 16 * E)
            indices(0)
            for k in range(J):
                gather(gate_tile(0, k))

            def batch_results(b, first, last):
                for k in range(J):
                    n, j = b * J + k, gate_tile(b, k)
                    pool.wait_ge(y_here[j], 16 * (b + 1))
                    if pool_scales(k):
                        pool.wait_ge(gate_ok, n + 1)
                        tt(y_got[:, j, :], y_got[:, j, :], gate_at(b, k), ALU.mult).then_inc(scaled_pool, 1)
                        pool.wait_ge(scaled_pool, scaled_at(b, k))
                    else:
                        pool.wait_ge(scaled, scaled_at(b, k))
                    if not (first and k < RES):
                        pool.wait_ge(stored[k % RES], 16 * (b * (J // RES) + k // RES))
                    settle()
                    tt(res[:, k % RES, :], y_got[:, j, :], tile(b, j), ALU.add).then_inc(res_ok, 1)
                    if not last:
                        settle()
                        nc.gpsimd.tensor_copy(idx_now[:, j:j + 1], gath_idx[:, bass.ds((b + 1) * J + j, 1)]
                                              ).then_inc(idx_copied, 1)
                        pool.wait_ge(idx_copied, B + 1 + n + 1)
                        pool.wait_ge(res_ok, n + 1)
                        settle()
                        gather(j)

            batch_results(0, True, False)
            with pool.Fori(1, B - 1) as b:
                batch_results(b, False, False)
            batch_results(B - 1, False, True)

        @block.tensor
        def _(pe):
            def mm3(out, l_hi, l_lo, r_hi, r_lo, start, stop):
                nc.tensor.matmul(out, l_hi, r_hi, start=start, stop=False)
                nc.tensor.matmul(out, l_hi, r_lo, start=False, stop=False)
                return nc.tensor.matmul(out, l_lo, r_hi, start=False, stop=stop)

            pe.wait_ge(consts_ok, 1)
            for k in range(2 * DC):
                if k % DC == 0:
                    pe.wait_ge((ld_wq, ld_wk)[k // DC], 16)
                if k >= 3:
                    pe.wait_ge(tr_lo, k - 2)
                raw = (wq_raw, wk_raw)[k // DC]
                for c in range(DC):
                    op = nc.tensor.transpose(tr_bank(k)[:, c * P:(c + 1) * P],
                                             raw[:, c, (k % DC) * P:(k % DC + 1) * P], ident[:])
                op.then_inc(tr_done, 1)
            def transpose_x(b, p, first):
                pe.wait_ge(ld_x, 16 * (2 * b + p + 1))
                for c in range(DC):
                    if c == 0 and p == 0 and not first:
                        pe.wait_ge(exp_done, b * J)
                        pe.wait_ge(row_ok, b)
                    pe.wait_ge(tr_lo, TR(b, DC * p + c) - 3)
                    for t in range(JH):
                        op = nc.tensor.transpose(tr_bank(TR0 + DC * p + c)[:, t * P:(t + 1) * P],
                                                 x_in[:, t, c * P:(c + 1) * P], ident[:])
                    op.then_inc(tr_done, 1)

            transpose_x(0, 0, True)
            pe.wait_ge(ld_small, 16 * 6)
            nc.tensor.transpose(misc_ps[:, 0:DC], bq4[:], ident[0:DC, 0:DC])
            for c in range(DC):
                op = nc.tensor.transpose(misc_ps[:, DC + c * B:DC + (c + 1) * B], cond4[:, c * P:(c + 1) * P],
                                         ident[0:B, 0:B])
            op.then_inc(misc_done, 1)
            pe.wait_ge(tr_lo, TR0)
            for t in range(DC):
                if t >= 2:
                    pe.wait_ge(out_free, t - 1)
                for c in range(DC):
                    op = mm3(out_bank(t), wqT_hi[:, c, t * P:(t + 1) * P], wqT_lo[:, c, t * P:(t + 1) * P],
                             wkT_hi[:, c, :], wkT_lo[:, c, :], c == 0, c == DC - 1)
                op.then_inc(out_done, 1)
            pe.wait_ge(tot_ok, 1)
            nc.tensor.matmul(counts_ps, upper[:], tot[:].rearrange("p b e -> p (b e)"), start=True, stop=False)
            nc.tensor.matmul(counts_ps, ones[:], earlier[:].rearrange("p b e -> p (b e)"), start=False, stop=True
                             ).then_inc(earlier_done, 1)
            pe.wait_ge(misc_ok, 2)
            pe.wait_ge(out_free, 3)
            for t in range(DC):
                for c in range(DC):
                    op = mm3(out_bank(4)[:, 2 * t:2 * t + 2], wkT_hi[:, c, t * P:(t + 1) * P],
                             wkT_lo[:, c, t * P:(t + 1) * P], bq_hi[:, c, :], bq_lo[:, c, :], c == 0, c == DC - 1)
            op.then_inc(out_done, 1)
            pe.wait_ge(out_free, 4)
            pe.wait_ge(ld_wv1, 16)
            for c in range(DC):
                op = nc.tensor.matmul(out_bank(5)[0:B, :], condT[:, c, :], wv1_raw[:, c, :],
                                      start=(c == 0), stop=(c == DC - 1))
            op.then_inc(out_done, 1)

            def z_tiles(b, p):
                k0, h = 15 if p else 0, half(p)
                pe.wait_ge(tr_lo, TR(b, DC * (p + 1) - 1) + 1)
                for t in range(DC):
                    pe.wait_ge(out_free, OUT(b, k0 + t) - 1)
                    for c in range(DC):
                        op = mm3(out_bank(OUT0 + k0 + t), m_hi[:, c, t * P:(t + 1) * P], m_lo[:, c, t * P:(t + 1) * P],
                                 xT_hi[:, c, h * SH:(h + 1) * SH], xT_lo[:, c, h * SH:(h + 1) * SH],
                                 c == 0, c == DC - 1)
                    op.then_inc(out_done, 1)

            def v_tiles(b):
                for j in range(J):
                    pe.wait_ge(out_free, OUT(b, DC + j) - 1)
                    for c in range(DC):
                        op = mm3(out_bank(OUT0 + DC + j), xT_hi[:, c, j * P:(j + 1) * P], xT_lo[:, c, j * P:(j + 1) * P],
                                 wv_hi[:, c, :], wv_lo[:, c, :], c == 0, c == DC - 1)
                    op.then_inc(out_done, 1)

            def scores(b, i):
                q = (i % JH) * P
                if i:
                    pe.wait_ge(exp_done, b * J + i)
                for k in range(2):
                    for c in range(DC):
                        if i % JH == 0 and k == 0:
                            pe.wait_ge(out_free, OUT(b, (15 if i else 0) + c) + 1)
                        if i == 0 and k == 0 and c == 0:
                            pe.wait_ge(tr_lo, TR(b, 2 * DC - 1) + 1)
                        op = mm3(ps[:, k, :], z_hi[:, c, q:q + P], z_lo[:, c, q:q + P],
                                 xT_hi[:, c, k * SH:(k + 1) * SH], xT_lo[:, c, k * SH:(k + 1) * SH],
                                 c == 0, c == DC - 1)
                op.then_inc(s_done, 1)

            def values(b, i):
                pe.wait_ge(out_free, PV(b, i) - 1)
                for j in range(J):
                    if j % JH == 0:
                        pe.wait_ge(p_lo, 2 * (b * J + i) + j // JH + 1)
                    if i == 0 and j == 0:
                        pe.wait_ge(out_free, OUT(b, 2 * DC + JH - 1) + 1)
                    op = mm3(out_bank(PV(0, i)), pT_hi[:, j, :], pT_lo[:, j, :], v_hi[:, j, :], v_lo[:, j, :],
                             j == 0, j == J - 1)
                op.then_inc(out_done, 1)

            def mean_row(b):
                pe.wait_ge(vsum_step, (2 * J - 1) * (b + 1))
                pe.wait_ge(mean_ok, 1)
                nc.tensor.matmul(row_ps, mean_w[:], dx[:], start=True, stop=True).then_inc(row_done, 1)

            def batch(b, first):
                if not first:
                    transpose_x(b, 0, first)
                    values(b - 1, J - 1)
                transpose_x(b, 1, first)
                z_tiles(b, 0)
                scores(b, 0)
                if first:
                    pe.wait_ge(wv_lo_ok, 1)
                v_tiles(b)
                for i in range(1, J):
                    scores(b, i)
                    values(b, i - 1)
                    if i == 3:
                        mean_row(b)
                    if i == JH - 1:
                        z_tiles(b, 1)

            batch(0, True)
            with pe.Fori(1, B) as b:
                batch(b, False)
            values(B - 1, J - 1)

            pe.wait_ge(ld_wr, 16)
            pe.wait_ge(row_ok, B)
            for g in range(DC):
                if g >= 2:
                    pe.wait_ge(t_lo, g - 1)
                for c in range(DC):
                    op = nc.tensor.transpose(ps[:, g % 2, c * P:(c + 1) * P], wr_raw[:, c, g * P:(g + 1) * P], ident[:])
                op.then_inc(t_done, 1)

            def transpose_xr(n, k, rows, first):
                pe.wait_ge(xr_ok, n + 1)
                if not (first and k < 2):
                    pe.wait_ge(g_t_lo, n - 1)
                for c in range(DC):
                    op = nc.tensor.transpose(ps[:, k % 2, c * P:(c + 1) * P], rows[:, k % 2, c * P:(c + 1) * P],
                                             ident[:])
                op.then_inc(g_t_done, 1)

            def gate_product(n, k, first):
                pe.wait_ge(g_t_lo, n + 1)
                if not (first and k < 2):
                    pe.wait_ge(gate_ok, n - 1)
                for c in range(DC):
                    op = mm3(ps[:, 6 + k % 2, :], xrT_hi[:, k % 2, c * P:(c + 1) * P], xrT_lo[:, k % 2, c * P:(c + 1) * P],
                             wrT_hi[:, c, :], wrT_lo[:, c, :], c == 0, c == DC - 1)
                op.then_inc(g_done, 1)

            pe.wait_ge(out_free, PV(B - 1, J - 1) + 1)
            pe.wait_ge(t_lo, DC)
            transpose_xr(0, 0, xr_early, True)
            for k in range(1, EARLY):
                transpose_xr(k, k, xr_early, True)
                gate_product(k - 1, k - 1, True)
            gate_product(EARLY - 1, EARLY - 1, True)

            def transpose_rows(e):
                pe.wait_ge(ld_xrow, 16 * (e + 1))
                pe.wait_ge(g_t_lo, EARLY)
                for g in range(2):
                    for c in range(2):
                        for t in range(CT):
                            op = nc.tensor.transpose(ps[:, g, c * CAP + t * P:c * CAP + (t + 1) * P],
                                                     xrow[:, t, (2 * g + c) * P:(2 * g + c + 1) * P], ident[:])
                    op.then_inc(t_done, 1)

            def hidden(e, first):
                for f in range(FC):
                    u = f // 2
                    if f % 2 == 0:
                        pe.wait_ge(w_lo, W(e, u) + 1)
                    if not (first and f < 4):
                        pe.wait_ge(relu_ok, FC * e + f - 3)
                    for c in range(DC):
                        if f == 0 and c % 2 == 0:
                            pe.wait_ge(t_lo, MT(e, c // 2) + 1)
                        at = c * CAP + (f % 2) * P
                        op = mm3(ps[:, 2 + f % 4, 0:CAP], wu_hi[:, u, at:at + P], wu_lo[:, u, at:at + P],
                                 xe_hi[:, c, :], xe_lo[:, c, :], c == 0, c == DC - 1)
                    op.then_inc(h_done, 1)

            def expert_out_half(e, t):
                for f in range(FC):
                    u = KU + f // 2
                    if t == 0:
                        pe.wait_ge(h_lo_ok, FC * e + f + 1)
                        if f % 2 == 0:
                            pe.wait_ge(w_lo, W(e, u) + 1)
                    at = (f % 2) * D
                    op = mm3(ps[:, 6 + t, :], h_hi[:, f, t * P:(t + 1) * P], h_lo[:, f, t * P:(t + 1) * P],
                             wu_hi[:, u, at:at + D], wu_lo[:, u, at:at + D], f == 0, f == FC - 1)
                    if t == CT - 1 and f % 2 and f < FC - 1:
                        op.then_inc(v_used, 1)
                op.then_inc(y_done, 1)

            def expert_out(e):
                for t in range(CT):
                    expert_out_half(e, t)

            transpose_rows(0)
            hidden(0, True)
            pe.wait_ge(gate_ok, EARLY)
            with pe.Fori(1, E) as e:
                expert_out(e - 1)
                hidden(e, False)
                pe.wait_ge(y_copied, CT * e)

            expert_out_half(E - 1, 0)
            transpose_xr(EARLY, EARLY, xr, True)
            expert_out_half(E - 1, 1)
            pe.wait_ge(y_copied, CT * E)
            with pe.Fori(1, NT // 4) as q:
                for k in range(4):
                    transpose_xr(4 * q + k, k, xr, False)
                    gate_product(4 * q + k - 1, (k - 1) % 4, False)
            gate_product(NT - 1, 3, False)


_INS = {"x": "x", "cond": "cond_1024", "tok": "itok_BxS_2_50255", "Wq2": "L0_cond_Wq2", "bq2": "L0_cond_bq2",
        "Wk2": "L0_cond_Wk2", "Wv": "L0_cond_Wv", "bv": "L0_cond_bv", "alpha": "L0_cond_alpha",
        "mk": "L1_cond_time_maa_k", "mr": "L1_cond_time_maa_r", "w_recept": "L1_cond_w_recept",
        "w_key": "L1_cond_w_key", "w_value": "L1_cond_w_value"}


def kernel(**inputs):
    import numpy as _np
    import concourse.bacc as _bacc
    from concourse import mybir as _mybir
    from concourse.bass_utils import run_bass_kernel_spmd as _run

    nc = _bacc.Bacc("TRN2", target_bir_lowering=False, num_devices=1, dynamic_dma_scratch_size=4096)
    arrays, args = {}, {}
    for short, name in _INS.items():
        a = _np.ascontiguousarray(inputs[name])
        arrays[f"in_{name}"] = a
        args[short] = nc.dram_tensor(f"in_{name}", a.shape, _mybir.dt.from_np(a.dtype), kind="ExternalInput").ap()
    args["out"] = nc.dram_tensor("out_0", inputs["x"].shape, _mybir.dt.float32, kind="ExternalOutput").ap()
    build(nc, args)
    r = _run(nc, [arrays], core_ids=[0])
    return r.results[0]["out_0"]
```

```python
from contextlib import ExitStack

import concourse.bass as bass
from concourse import mybir

F32 = mybir.dt.float32
F32R = mybir.dt.float32r
I32 = mybir.dt.int32
U32 = mybir.dt.uint32
ACT = mybir.ActivationFunctionType
ALU = mybir.AluOpType
AX = mybir.AxisListType

P = 128
HASH_PRIME = 5099
MIN_CAPACITY = 4


def build(nc, A):
    B, S, D = A["x"].shape
    E, _, F = A["w_key"].shape
    N = B * S
    CAP = max(MIN_CAPACITY, N // E)
    DC = D // P
    J = S // P
    JH = J // 2
    SH = S // 2
    FC = F // P
    CT = CAP // P
    NT = B * J
    SCALE = 1.0 / float(D) ** 0.5
    RAW = 4
    UNITS = 8
    KU = UNITS // 2
    RES = 8
    POOL_UNITS = (2, 3)
    DVE_SQUARE = 5
    EARLY = 4
    assert (D, J, FC, CT, E) == (512, 8, 8, 2, 16)

    xk_dram = nc.dram_tensor("xk_slots", (2 * N, D), F32, kind="Internal").ap()
    y_dram = nc.dram_tensor("y_slots", (N + 1, D), F32, kind="Internal").ap()
    shift_dram = nc.dram_tensor("shifted", (B, P + 1, D), F32, kind="Internal").ap()
    crow_dram = nc.dram_tensor("cond_rows", (B, D), F32, kind="Internal").ap()
    x_v = A["x"].rearrange("b (p j) d -> b p (j d)", p=P)
    out_v = A["out"].rearrange("b (p j) d -> b p (j d)", p=P)
    wkey_v = A["w_key"].rearrange("e (c p) f -> e p c f", p=P)
    wval_v = A["w_value"].rearrange("e (k p) d -> e p k d", p=P)

    with ExitStack() as ctx:
        def sem(name):
            return ctx.enter_context(nc.semaphore(name))

        def alloc(stack):
            return lambda name, shape, dt: stack.enter_context(nc.sbuf_tensor(name, shape, dt))

        sb = alloc(ctx)
        ident = sb("ident", [P, P], F32)
        mean_w = sb("mean_w", [P, P], F32)
        mk_row = sb("mk_row", [P, D], F32)
        mr_row = sb("mr_row", [P, D], F32)
        scat_idx = sb("scat_idx", [P, NT], I32)
        gath_idx = sb("gath_idx", [P, NT], I32)
        idx_now = sb("idx_now", [P, J], I32)
        dx = sb("dx", [P, D], F32)
        with ExitStack() as room:
            row_t = alloc(room)("row_t", [P, CT, D], F32)
        xk = sb("xk", [P, 2, D], F32)
        b_row = sb("b_row", [P, D], F32)
        x_before = sb("x_before", [P, D], F32)
        alpha = sb("alpha", [P, 1], F32)
        u_col = sb("u_col", [P, DC], F32)
        neg_max = sb("neg_max", [P, J], F32)
        row_sum = sb("row_sum", [P, J], F32)
        row_inv = sb("row_inv", [P, J], F32)

        with ExitStack() as room:
            sbs = alloc(room)
            wq_raw = sbs("wq_raw", [P, DC, D], F32)
            wk_raw = sbs("wk_raw", [P, DC, D], F32)
            wv2_raw = sbs("wv2_raw", [P, DC, D], F32)
            wqT_hi = sbs("wqT_hi", [P, DC, D], F32R)
            wqT_lo = sbs("wqT_lo", [P, DC, D], F32R)
            wkT_hi = sbs("wkT_hi", [P, DC, D], F32R)
            wkT_lo = sbs("wkT_lo", [P, DC, D], F32R)
            tok = sbs("tok", [P, NT], I32)
            e_int = sbs("e_int", [P, NT], I32)
            e_f = sbs("e_f", [P, NT], F32)
            own_i = sbs("own_i", [P, NT], I32)
            own_f = sbs("own_f", [P, NT], F32)
            onehot = sbs("onehot", [P, B, J, E], F32)
            rank = sbs("rank", [P, B, J, E], F32)
            tot = sbs("tot", [P, B, E], F32)
            earlier = sbs("earlier", [P, B, E], F32)
            pos = sbs("pos", [P, NT], F32)
            keep = sbs("keep", [P, NT], F32)
            slot = sbs("slot", [P, NT], F32)
            diff = sbs("diff", [P, NT], F32)
        x1 = sb("x1", [P, NT * D], F32)

        with ExitStack() as room:
            sba = alloc(room)
            x_in = sba("x_in", [P, JH, D], F32)
            m_hi = sba("m_hi", [P, DC, D], F32R)
            m_lo = sba("m_lo", [P, DC, D], F32R)
            wv_hi = sba("wv_hi", [P, DC, D], F32R)
            wv_lo = sba("wv_lo", [P, DC, D], F32R)
            xT_hi = sba("xT_hi", [P, DC, S], F32R)
            xT_lo = sba("xT_lo", [P, DC, S], F32R)
            z_hi = sba("z_hi", [P, DC, SH], F32R)
            z_lo = sba("z_lo", [P, DC, SH], F32R)
            prob = sba("prob", [P, S], F32)
            prob_t = sba("prob_t", [P, S], F32)
            pT_hi = sba("pT_hi", [P, J, P], F32R)
            pT_lo = sba("pT_lo", [P, J, P], F32R)
            with ExitStack() as inner:
                sbs = alloc(inner)
                wv1_raw = sbs("wv1_raw", [P, DC, D], F32)
                upper = sbs("upper", [P, P], F32)
                ones = sbs("ones", [P, P], F32)
                cond4 = sbs("cond4", [B, D], F32)
                bq_row = sbs("bq_row", [P, D], F32)
                wk_bq = sbs("wk_bq", [P, DC, D], F32)
                warm = sbs("warm", [P, 1], F32)
                condT = sbs("condT", [P, DC, B], F32)
                bv4 = sbs("bv4", [B, D], F32)
                crow4 = sbs("crow4", [B, D], F32)
                rest = sbs("rest", [P, 1], F32)
            v_hi = sba("v_hi", [P, J, D], F32R)
            v_lo = sba("v_lo", [P, J, D], F32R)

        with ExitStack() as room:
            sbm = alloc(room)
            w_raw = sbm("w_raw", [P, RAW, 2 * D], F32)
            wrT_hi = sbm("wrT_hi", [P, DC, D], F32R)
            wrT_lo = sbm("wrT_lo", [P, DC, D], F32R)
            with ExitStack() as inner:
                sbf = alloc(inner)
                y_got = sbf("y_got", [P, J, D], F32)
                res = sbf("res", [P, RES, D], F32)
                gate = sbf("gate", [P, J, D], F32)
            with ExitStack() as inner:
                sbf = alloc(inner)
                sbf("first_units", [P, KU, 2 * D], F32)
                wr_raw = sbf("wr_raw", [P, DC, D], F32)
            wu_hi = sbm("wu_hi", [P, UNITS, 2 * D], F32R)
            wu_lo = sbm("wu_lo", [P, UNITS, 2 * D], F32R)
            with ExitStack() as inner:
                sbf = alloc(inner)
                xrT_hi = sbf("xrT_hi", [P, 2, D], F32R)
                xrT_lo = sbf("xrT_lo", [P, 2, D], F32R)
            xe_hi = sbm("xe_hi", [P, DC, CAP], F32R)
            xe_lo = sbm("xe_lo", [P, DC, CAP], F32R)
            h_hi = sbm("h_hi", [P, FC, CAP], F32R)
            h_lo = sbm("h_lo", [P, FC, CAP], F32R)
            xrow = sbm("xrow", [P, CT, D], F32)
            with ExitStack() as inner:
                xr = alloc(inner)("xr", [P, 2, D], F32)
            relu = sbm("relu", [P, 2, CAP], F32)
            hsq = sbm("hsq", [P, 2, CAP], F32)
            y_out = sbm("y_out", [P, CT, D], F32)
            with ExitStack() as inner:
                sbf = alloc(inner)
                sbf("first_gates", [P, EARLY - 2, D], F32)
                xr_early = sbf("xr_early", [P, 2, D], F32)
            gate_early = sbm("gate_early", [P, EARLY, D], F32)

        ps = ctx.enter_context(nc.psum_tensor("ps", [P, 8, 512], F32))
        score_ps = ps[:, 0:2, :].rearrange("p a n -> p (a n)")
        row_ps = ps[:, 5, :]
        misc_ps = ps[:, 2, :]
        counts_ps = ps[:, 3, 0:B * E]

        def tr_bank(n):
            return ps[:, n if n < TR0 else (0, 1, 4, 5)[(n - TR0) % 4], :]

        def p_bank(g):
            return ps[:, 2 + g, :]

        def out_bank(n):
            return ps[:, 6 + n % 2, :]

        ld_wqk = [sem(f"ld_wqk{i}") for i in range(4)]
        ld_x, ld_wv2, ld_wv1 = (sem(n) for n in ("ld_x", "ld_wv2", "ld_wv1"))
        ld_tok, ld_small, ld_x1, ld_brow, ld_wr, ld_before = (
            sem(n) for n in ("ld_tok", "ld_small", "ld_x1", "ld_brow", "ld_wr", "ld_before"))
        ld_raw = [sem(f"ld_raw{i}") for i in range(RAW)]
        ld_xrow = sem("ld_xrow")
        consts_ok, own_ok, tot_ok, earlier_done, index_ok = (
            sem(n) for n in ("consts_ok", "own_ok", "tot_ok", "earlier_done", "index_ok"))
        misc_done, misc_ok, u_ok = sem("misc_done"), sem("misc_ok"), sem("u_ok")
        mean_ok, wv_hi_ok, wv_lo_ok, crow_ok, crow_stored = (
            sem(n) for n in ("mean_ok", "wv_hi_ok", "wv_lo_ok", "crow_ok", "crow_stored"))
        zeroed, zero_row, cond_rows = sem("zeroed"), sem("zero_row"), sem("cond_rows")
        tr_done, tr_hi, tr_lo = sem("tr_done"), sem("tr_hi"), sem("tr_lo")
        p_blocks, p_act, p_dve, p_hi, p_lo = (sem(n) for n in ("p_blocks", "p_act", "p_dve", "p_hi", "p_lo"))
        p_act_half, p_dve_half = sem("p_act_half"), sem("p_dve_half")
        out_done, out_hi, out_free = sem("out_done"), sem("out_hi"), sem("out_free")
        s_done, max_done, exp_done = sem("s_done"), sem("max_done"), sem("exp_done")
        row_done, row_ok, x1_ok = sem("row_done"), sem("row_ok"), sem("x1_ok")
        shift_out, shift_in = sem("shift_out"), sem("shift_in")
        scattered = [sem(f"scattered{i}") for i in range(2)]
        t_done, t_hi, t_lo = sem("t_done"), sem("t_hi"), sem("t_lo")
        r_blocks, r_act, r_dve = sem("r_blocks"), sem("r_act"), sem("r_dve")
        v_used, w_hi, w_lo, w_lo_pool = sem("v_used"), sem("w_hi"), sem("w_lo"), sem("w_lo_pool")
        h_done, relu_ok, h_hi_ok, h_lo_ok = sem("h_done"), sem("relu_ok"), sem("h_hi_ok"), sem("h_lo_ok")
        y_done, y_copied = sem("y_done"), sem("y_copied")
        y_stored = [sem(f"y_stored{i}") for i in range(CT)]
        xr_ok, g_t_done, g_t_hi, g_t_lo = sem("xr_ok"), sem("g_t_done"), sem("g_t_hi"), sem("g_t_lo")
        g_done, gate_ok, res_ok = sem("g_done"), sem("gate_ok"), sem("res_ok")
        y_here = [sem(f"y_here{i}") for i in range(J)]
        stored = [sem(f"stored{i}") for i in range(RES)]
        settled = sem("settled")
        dve_chain, pool_chain = sem("dve_chain"), sem("pool_chain")
        inv_ok, xr_sub, xr_mul = sem("inv_ok"), sem("xr_sub"), sem("xr_mul")
        vsum_step, xk_step, idx_copied, hsq_ok, scaled, scaled_pool = (
            sem(n) for n in ("vsum_step", "xk_step", "idx_copied", "hsq_ok", "scaled", "scaled_pool"))
        xk_last = sem("xk_last")
        x1_last, hsq_dve = sem("x1_last"), sem("hsq_dve")
        res_end = sem("res_end")

        TR0, OUT0, HI0 = 8, 5, 4

        def TR(b, k):
            return TR0 + 2 * DC * b + k

        def OUT(b, k):
            return OUT0 + 24 * b + k

        def PV(b, i):
            return OUT(b, 12 + i if i < 3 else 16 + i)

        def HI(b, k):
            return HI0 + 16 * b + k

        def WH(e, u):
            return UNITS * e + u

        def WL(e, u):
            return UNITS * e + u - (len(POOL_UNITS) if not isinstance(e, int) or e or u > max(POOL_UNITS) else 0)

        def wait_lo(engine, e, u):
            if isinstance(e, int) and e == 0 and u in POOL_UNITS:
                engine.wait_ge(w_lo_pool, POOL_UNITS.index(u) + 1)
            else:
                engine.wait_ge(w_lo, WL(e, u) + 1)

        def MT(e, g):
            return DC + 2 * e + g

        def half(p):
            return 1 - p

        def query(i):
            return (i + JH) % J

        POOL_SCALES = (3, 7)
        ENDS = 4

        def gate_t_bank(k):
            return ps[:, 2 + k % 2, :]

        def gate_bank(k):
            return ps[:, 7 - k % 2, :]

        def block_move(a, c, g=None):
            if g is not None:
                return (p_bank(g)[32 * c:32 * c + 32, :].rearrange("p (k a n) -> p k a n", a=4, n=32)[:, :, a, :],
                        prob_t[32 * a:32 * a + 32, g * SH:(g + 1) * SH].rearrange("p (k c n) -> p k c n", c=4, n=32)
                        [:, :, c, :])
            return (ps[32 * c:32 * c + 32, 2:4, :].rearrange("p g (k a n) -> p (g k) a n", a=4, n=32)[:, :, a, :],
                    prob_t[32 * a:32 * a + 32, :].rearrange("p (k c n) -> p k c n", c=4, n=32)[:, :, c, :])

        def row_move(a, c):
            return (ps[32 * c:32 * c + 32, 0:2, :].rearrange("p g (k t a n) -> p (g k) t a n", t=CT, a=4, n=32)
                    [:, :, :, a, :],
                    row_t[32 * a:32 * a + 32, :, :].rearrange("p t (k c n) -> p k t c n", c=4, n=32)[:, :, :, c, :])

        def gate_tile(b, k):
            return k if not isinstance(b, int) or b or k > EARLY else (k + 1) % (EARLY + 1)

        def pool_scales(k):
            return k in POOL_SCALES

        def scaled_at(b, k):
            mine = [i for i in range(J) if pool_scales(i) == pool_scales(k)]
            return len(mine) * b + mine.index(k) + 1

        def gate_at(b, k):
            return gate_early[:, k, :] if isinstance(b, int) and b == 0 and k < EARLY else gate[:, k, :]

        def tile(b, j):
            return x1[:, bass.ds((b * J + j) * D, D)]

        def batch_of(view, b):
            return view[b] if isinstance(b, int) else view[bass.ds(b, 1)].rearrange("a p n -> (a p) n")

        block = ctx.enter_context(nc.Block())

        @block.sync
        def _(sp):
            x_in_flat = x_in[:].rearrange("p j d -> p (j d)")
            for i, sem_half in enumerate(ld_wqk):
                raw, name, h = (wq_raw, wk_raw)[i // 2], ("Wq2", "Wk2")[i // 2], i % 2 * (D // 2)
                sp.dma_start(raw[:, :, h:h + D // 2], A[name][:, h:h + D // 2].rearrange("(c p) e -> p c e", p=P)
                             ).then_inc(sem_half, 16)
            sp.dma_start(x_in_flat, x_v[0][:, half(0) * JH * D:(half(0) + 1) * JH * D]).then_inc(ld_x, 16)
            sp.dma_start(tok[:].rearrange("p (b j) -> p b j", b=B),
                         A["tok"].rearrange("b (p j) -> p b j", p=P)).then_inc(ld_tok, 16)
            for dst, src in ((cond4[:], A["cond"]),
                             (alpha[:], A["alpha"].rearrange("(a d) -> a d", a=1).partition_broadcast(P)),
                             (bq_row[:], A["bq2"].rearrange("(a d) -> a d", a=1).partition_broadcast(P)),
                             (bv4[:], A["bv"].rearrange("(a d) -> a d", a=1).partition_broadcast(B)),
                             (mk_row[:], A["mk"].rearrange("(a d) -> a d", a=1).partition_broadcast(P)),
                             (mr_row[:], A["mr"].rearrange("(a d) -> a d", a=1).partition_broadcast(P))):
                sp.dma_start(dst, src).then_inc(ld_small, 16)
            sp.dma_start(wv1_raw[:], A["Wv"][0:D, :].rearrange("(c p) e -> p c e", p=P)).then_inc(ld_wv1, 16)

            def load_half(b, p, after):
                h = half(p)
                sp.wait_ge(tr_done, after + 1)
                sp.dma_start(x_in_flat, batch_of(x_v, b)[:, h * JH * D:(h + 1) * JH * D]).then_inc(ld_x, 16)

            def load_residual(b):
                sp.dma_start(x1[:, bass.ds(b * J * D, J * D)], batch_of(x_v, b)).then_inc(ld_x1, 16)

            def load_row(b):
                sp.dma_start(b_row[:], crow_dram[bass.ds(b, 1), :].partition_broadcast(P)).then_inc(ld_brow, 16)

            load_half(0, 1, TR(0, 3))
            sp.dma_start(wv2_raw[:], A["Wv"][D:2 * D, :].rearrange("(c p) e -> p c e", p=P)).then_inc(ld_wv2, 16)
            sp.wait_ge(crow_ok, 1)
            sp.dma_start(crow_dram, crow4[:]).then_inc(crow_stored, 16)
            load_half(1, 0, TR(0, 7))
            sp.wait_ge(wv_lo_ok, 1)
            load_residual(0)
            sp.wait_ge(crow_stored, 16)
            load_row(0)
            sp.wait_ge(consts_ok, 1)
            sp.dma_start(xk_dram[0:N, :].rearrange("(p r) d -> p r d", p=P),
                         dx[:].unsqueeze(1).broadcast_to((P, N // P, D))).then_inc(zeroed, 16)

            def batch_loads(b, last):
                load_half(b, 1, TR(b, 3))
                if not last:
                    load_half(b + 1, 0, TR(b, 7))
                sp.wait_ge(ld_x1, 16 * b)
                if last:
                    sp.wait_ge(index_ok, 1)
                load_residual(b)
                sp.wait_ge(x1_ok, J * b)
                load_row(b)

            with sp.Fori(1, B - 1) as b:
                batch_loads(b, False)
            batch_loads(B - 1, True)

            def load_unit(e, u):
                if u < KU:
                    src = wkey_v[bass.ds(e, 1), :, :, u * CAP:(u + 1) * CAP].rearrange("a p c f -> (a p) c f")
                    dst = w_raw[:, u % RAW, :].rearrange("p (c f) -> p c f", c=DC)
                else:
                    v = 2 * (u - KU)
                    src = wval_v[bass.ds(e, 1), :, v:v + 2, :].rearrange("a p k d -> (a p) k d")
                    dst = w_raw[:, u % RAW, :].rearrange("p (k d) -> p k d", k=2)
                sp.dma_start(dst, src).then_inc(ld_raw[u % RAW], 16)

            def load_rows(e):
                sp.dma_start(xrow[:], xk_dram[bass.ds(e * CAP, CAP), :].rearrange("(t p) d -> p t d", p=P)
                             ).then_inc(ld_xrow, 16)

            sp.wait_ge(out_done, OUT(B - 1, 18) + 1)
            for u in range(RAW):
                load_unit(0, u)
            sp.wait_ge(s_done, B * J)
            sp.dma_start(wr_raw[:], A["w_recept"].rearrange("(c p) d -> p c d", p=P)).then_inc(ld_wr, 16)
            for q in scattered:
                sp.wait_ge(q, 16 * NT // 2)
            load_rows(0)

            def load_before(b):
                sp.dma_start(x_before[:], batch_of(shift_dram[:, 0:P, :], b)).then_inc(ld_before, 16)

            load_before(0)

            def expert_loads(e, first, last):
                if not last:
                    sp.wait_ge(*((t_done, MT(0, 1) + 1) if first else (r_blocks, e)))
                    load_rows(e + 1)
                for u in range(RAW if first else 0, UNITS):
                    wait_lo(sp, *((e, u - RAW) if u >= RAW else (e - 1, u - RAW + UNITS)))
                    load_unit(e, u)

            expert_loads(0, True, False)
            with sp.Fori(1, E - 1) as e:
                expert_loads(e, False, False)
            expert_loads(E - 1, False, True)

            def batch_results(b, ahead, last=False):
                for k in range(J - ENDS if last else J):
                    j = gate_tile(b, k)
                    sp.wait_ge(res_ok, b * J + k + 1)
                    sp.dma_start(batch_of(out_v, b)[:, j * D:(j + 1) * D], res[:, k % RES, :]
                                 ).then_inc(stored[k % RES], 16)
                    if k == JH and ahead:
                        sp.wait_ge(xr_ok, (b + 1) * J + 1)
                        load_before(b + 2)

            sp.wait_ge(xr_ok, EARLY + 1)
            load_before(1)
            batch_results(0, True)
            with sp.Fori(1, B - 2) as b:
                batch_results(b, True)
            batch_results(B - 2, False)
            batch_results(B - 1, False, True)
            for q in stored:
                sp.wait_ge(q, 16 * NT // RES)

        @block.scalar
        def _(act):
            def hi(out, in_, done, bias=0.0, scale=1.0, func=ACT.Copy):
                nc.scalar.activation(out, in_, func, bias=bias, scale=scale).then_inc(done, 1)

            def tr_split(n, out):
                act.wait_ge(tr_done, n + 1)
                hi(out, tr_bank(n), tr_hi)

            act.wait_ge(consts_ok, 1)
            nc.scalar.activation(warm[:], ident[:, 0:1], ACT.Copy)
            for k in range(2 * DC):
                tr_split(k, (wqT_hi, wkT_hi)[k // DC][:, k % DC, :])

            def x_split(b, p):
                h = half(p)
                for c in range(DC):
                    act.wait_ge(tr_done, TR(b, DC * p + c) + 1)
                    hi(xT_hi[:, c, h * SH:(h + 1) * SH], tr_bank(TR0 + DC * p + c), tr_hi)

            x_split(0, 0)
            for k in range(DC):
                act.wait_ge(out_done, k + 1)
                hi(m_hi[:, k, :], out_bank(k), out_hi, scale=SCALE)

            def z_split(b, k0):
                for c in range(DC):
                    act.wait_ge(out_done, OUT(b, k0 + c) + 1)
                    hi(z_hi[:, c, :], out_bank(OUT0 + k0 + c), out_hi, bias=u_col[:, c:c + 1], func=ACT.Identity)

            def p_move(j, g=None):
                out, in_ = block_move(j % 4, j // 4, g)
                op = nc.scalar.activation(out, in_, ACT.Copy)
                if j == J - 1:
                    op.then_inc(p_act if g != 0 else p_act_half, 1)

            def p_hi_part(g):
                hi(pT_hi[:, JH * g:JH * (g + 1), :].rearrange("p a n -> p (a n)"), p_bank(g), p_hi)

            def batch(b, first):
                if not first:
                    x_split(b, 0)
                x_split(b, 1)
                if first:
                    act.wait_ge(u_ok, 1)
                z_split(b, 0)
                if first:
                    act.wait_ge(ld_wv2, 16)
                    nc.scalar.activation(wv_hi[:].rearrange("p c n -> p (c n)"),
                                         wv2_raw[:].rearrange("p c n -> p (c n)"), ACT.Copy).then_inc(wv_hi_ok, 1)
                for i in range(J):
                    act.wait_ge(max_done, b * J + i + 1)
                    nc.scalar.activation(prob[:], score_ps, ACT.Exp, bias=neg_max[:, i:i + 1],
                                         accum_out=row_sum[:, i:i + 1]).then_inc(exp_done, 1)
                    if not (first and i == 0):
                        act.wait_ge(p_lo, 2 * (b * J + i))
                    act.wait_ge(p_blocks, b * J + i + 1)
                    if i == 0:
                        for j in range(J):
                            p_move(j)
                            act.wait_ge(out_done, OUT(b, DC + j) + 1)
                            if j == 0:
                                act.wait_ge(vsum_step, (2 * J - 1) * b)
                                if first:
                                    act.wait_ge(crow_stored, 16)
                            hi(v_hi[:, j, :], out_bank(OUT0 + DC + j), out_hi)
                    elif i < J - 1:
                        for j in range(J):
                            p_move(j)
                        act.wait_ge(out_done, PV(b, i - 1) + 1)
                    else:
                        for j in range(J):
                            p_move(j, 0)
                        act.wait_ge(out_done, PV(b, i - 1) + 1)
                        act.wait_ge(p_act_half, b + 1)
                        act.wait_ge(p_dve_half, b + 1)
                        p_hi_part(0)
                        for j in range(J):
                            p_move(j, 1)
                    act.wait_ge(p_act, b * J + i + 1)
                    act.wait_ge(p_dve, b * J + i + 1)
                    for g in range(2) if i < J - 1 else (1,):
                        p_hi_part(g)
                    if i == JH - 1:
                        z_split(b, 15)

            batch(0, True)
            with act.Fori(1, B) as b:
                batch(b, False)

            def unit_split(e, u, first):
                act.wait_ge(ld_raw[u % RAW], 16 * (2 * e + u // RAW + 1))
                if first:
                    act.wait_ge(s_done, B * J)
                else:
                    if u < KU:
                        act.wait_ge(h_done, FC * (e - 1) + 2 * u + 2)
                    elif u < UNITS - 1:
                        act.wait_ge(v_used, (KU - 1) * (e - 1) + u - KU + 1)
                    else:
                        act.wait_ge(y_done, CT * e)
                hi(wu_hi[:, u, :], w_raw[:, u % RAW, :], w_hi)

            def row_moves(e):
                act.wait_ge(r_blocks, e)
                act.wait_ge(t_lo, MT(e, 0))
                for a in range(4):
                    op = nc.scalar.activation(*row_move(a, 3), ACT.Copy)
                op.then_inc(r_act, 1)

            def rows_split(e, first):
                if not first:
                    act.wait_ge(r_act, e)
                    act.wait_ge(r_dve, e)
                for g in range(2):
                    if first:
                        act.wait_ge(t_done, MT(e, g) + 1)
                    hi(xe_hi[:, 2 * g:2 * g + 2, :].rearrange("p a n -> p (a n)"), ps[:, g, :], t_hi)

            def copy_y_half(e, t):
                act.wait_ge(y_done, CT * e + t + 1)
                if not (isinstance(e, int) and e == 0):
                    act.wait_ge(y_stored[t], 16 * e)
                nc.scalar.activation(y_out[:, t, :], ps[:, 6 + t, :], ACT.Copy).then_inc(y_copied, 1)

            def copy_y(e):
                for t in range(CT):
                    copy_y_half(e, t)

            def hidden(e, first):
                for f in range(FC):
                    act.wait_ge(h_done, FC * e + f + 1)
                    if not (first and f < 2):
                        act.wait_ge(h_lo_ok, FC * e + f - 1)
                    nc.scalar.activation(relu[:, f % 2, :], ps[:, 2 + f % 4, 0:CAP], ACT.Relu).then_inc(relu_ok, 1)
                    act.wait_ge(relu_ok, FC * e + f + 1)
                    nc.scalar.activation(h_hi[:, f, :], relu[:, f % 2, :], ACT.Square).then_inc(h_hi_ok, 1)
                    if f % 2:
                        unit_split(e, KU + f // 2, first)
                    if first and f == 3:
                        row_moves(1)

            def gate_split(n, k, first):
                act.wait_ge(g_t_done, n + 1)
                if not (first and k < 2):
                    act.wait_ge(g_done, n - 1)
                hi(xrT_hi[:, k % 2, :], gate_t_bank(k), g_t_hi)

            def sigmoid(b, k, first):
                n = b * J + k
                act.wait_ge(g_done, n + 1)
                if not first:
                    act.wait_ge(scaled_pool if pool_scales(k) else scaled, scaled_at(b - 1, k))
                nc.scalar.activation(gate_at(b, k), gate_bank(k), ACT.Sigmoid).then_inc(gate_ok, 1)

            for g in range(DC):
                act.wait_ge(t_done, g + 1)
                hi(wrT_hi[:, g, :], tr_bank(TR0 + g), t_hi)
            for u in range(KU // 2):
                unit_split(0, u, True)
            gate_split(0, 0, True)
            for k in range(1, EARLY):
                gate_split(k, k, True)
                if k == 1:
                    for u in range(KU // 2, KU):
                        unit_split(0, u, True)
                sigmoid(0, k - 1, True)
            sigmoid(0, EARLY - 1, True)
            rows_split(0, True)
            hidden(0, True)

            def expert(e, last):
                rows_split(e, False)
                for u in range(KU):
                    unit_split(e, u, False)
                copy_y(e - 1)
                if not last:
                    row_moves(e + 1)
                hidden(e, False)

            expert(1, False)
            with act.Fori(2, E - 1) as e:
                expert(e, False)
            expert(E - 1, True)

            copy_y_half(E - 1, 0)
            gate_split(EARLY, EARLY, True)
            copy_y_half(E - 1, 1)
            for k in range(EARLY + 1, J):
                gate_split(k, k, True)
                sigmoid(0, k - 1, True)

            def gates(b, first):
                for k in range(J):
                    gate_split(b * J + k, k, False)
                    if k:
                        sigmoid(b, k - 1, False)
                    else:
                        sigmoid(b - 1, J - 1, first)

            gates(1, True)
            with act.Fori(2, B) as b:
                gates(b, False)
            sigmoid(B - 1, J - 1, False)
            for k in range(J - ENDS, J):
                act.wait_ge(res_end, k - (J - ENDS) + 1)
                act.dma_start(out_v[B - 1][:, k * D:(k + 1) * D], res[:, k % RES, :]).then_inc(stored[k % RES], 16)

        @block.vector
        def _(dve):
            chain = [0]

            def link(op):
                chain[0] += 1
                op.then_inc(dve_chain, 1)
                dve.wait_ge(dve_chain, chain[0])

            tt, ts, stt = nc.vector.tensor_tensor, nc.vector.tensor_scalar, nc.vector.scalar_tensor_tensor

            def lo(out, in_, hi_part, done):
                tt(out, in_, hi_part.bitcast(F32), ALU.subtract).then_inc(done, 1)

            for k in range(2 * DC):
                dve.wait_ge(tr_hi, k + 1)
                lo((wqT_lo, wkT_lo)[k // DC][:, k % DC, :], tr_bank(k), (wqT_hi, wkT_hi)[k // DC][:, k % DC, :], tr_lo)

            def x_split(b, p):
                h = half(p)
                for c in range(DC):
                    dve.wait_ge(tr_hi, TR(b, DC * p + c) + 1)
                    lo(xT_lo[:, c, h * SH:(h + 1) * SH], tr_bank(TR0 + DC * p + c),
                       xT_hi[:, c, h * SH:(h + 1) * SH], tr_lo)

            x_split(0, 0)

            def m_split(k):
                dve.wait_ge(out_hi, k + 1)
                stt(m_lo[:, k, :], out_bank(k), SCALE, m_hi[:, k, :].bitcast(F32), ALU.mult, ALU.subtract
                    ).then_inc(out_free, 1)

            m_split(0)
            dve.wait_ge(ld_small, 16 * 6)
            for t in range(DC):
                op = stt(wk_bq[:, t, :], wk_raw[:, t, :], SCALE, bq_row[:], ALU.mult, ALU.mult,
                         accum_out=u_col[:, t:t + 1])
            op.then_inc(u_ok, 1)
            dve.wait_ge(consts_ok, 1)
            link(ts(rest[:], alpha[:], -1.0, 1.0, ALU.mult, ALU.add))
            ts(mean_w[:], mean_w[:], alpha[:], None, ALU.mult).then_inc(mean_ok, 1)
            m_split(1)
            dve.wait_ge(ld_tok, 16)
            link(ts(e_int[:], tok[:], E - 1, None, ALU.bitwise_and))
            link(ts(tok[:], e_int[:], float(HASH_PRIME % E), None, ALU.mult))
            link(ts(e_int[:], tok[:], E - 1, None, ALU.bitwise_and))
            link(nc.vector.tensor_copy(e_f[:], e_int[:]))
            m_split(2)
            oh = onehot[:].rearrange("p b j e -> p (b j) e")
            for e in range(E):
                op = ts(oh[:, :, e], e_f[:], float(e), None, ALU.is_equal)
            link(op)
            dve.wait_ge(misc_done, 1)
            nc.vector.tensor_copy(condT[:].rearrange("p c b -> p (c b)"), misc_ps[:, 0:DC * B]).then_inc(misc_ok, 1)
            m_split(3)
            link(nc.vector.tensor_reduce(tot[:], onehot[:].rearrange("p b j e -> p b e j"), AX.X, ALU.add))
            link(nc.vector.memset(earlier[:], 0.0))
            for b in range(1, B - 1):
                link(tt(earlier[:, b, :], earlier[:, b - 1, :], tot[:, b - 1, :], ALU.add))
            tt(earlier[:, B - 1, :], earlier[:, B - 2, :], tot[:, B - 2, :], ALU.add).then_inc(tot_ok, 1)
            dve.wait_ge(out_done, OUT0)
            tt(crow4[:], out_bank(4)[0:B, :], bv4[:], ALU.add).then_inc(out_free, 1)
            dve.wait_ge(out_free, OUT0)
            ts(crow4[:], crow4[:], rest[0:B, :], None, ALU.mult).then_inc(crow_ok, 1)

            def token_slots():
                for j in range(1, J):
                    link(tt(rank[:, :, j, :], rank[:, :, j - 1, :], onehot[:, :, j - 1, :], ALU.add))
                rank_f = rank[:].rearrange("p b j e -> p (b j e)")
                link(tt(rank_f, rank_f, onehot[:].rearrange("p b j e -> p (b j e)"), ALU.mult))
                link(nc.vector.tensor_reduce(pos[:], rank[:].rearrange("p b j e -> p (b j) e"), AX.X, ALU.add))
                link(ts(keep[:], pos[:], float(CAP), None, ALU.is_lt))
                link(stt(slot[:], e_f[:], float(CAP), pos[:], ALU.mult, ALU.add))
                dve.wait_ge(own_ok, 1)
                link(nc.vector.tensor_copy(own_f[:], own_i[:]))
                link(tt(diff[:], slot[:], own_f[:], ALU.subtract))
                link(tt(diff[:], diff[:], keep[:], ALU.mult))
                link(tt(scat_idx[:], diff[:], own_f[:], ALU.add))
                link(ts(diff[:], slot[:], float(-N), None, ALU.add))
                link(tt(diff[:], diff[:], keep[:], ALU.mult))
                ts(gath_idx[:], diff[:], float(N), None, ALU.add).then_inc(index_ok, 1)

            def pv_evacuate(b, i):
                dve.wait_ge(out_done, PV(b, i) + 1)
                dve.wait_ge(ld_x1, 16 * (b + 1))
                dve.wait_ge(inv_ok, b * J + i + 1)
                row = tile(b, query(i))
                stt(row, out_bank(PV(0, i)), row_inv[:, i:i + 1], row, ALU.mult, ALU.add
                    ).then_inc(out_free, 1)

            def z_split(b, k0, h0):
                for c in range(DC):
                    dve.wait_ge(out_hi, HI(b, h0 + c) + 1)
                    stt(z_lo[:, c, :], out_bank(OUT0 + k0 + c), u_col[:, c:c + 1], z_hi[:, c, :].bitcast(F32),
                        ALU.add, ALU.subtract).then_inc(out_free, 1)

            def p_move(j, g=None):
                op = nc.vector.tensor_copy(*block_move(j % 4, 2 + j // 4, g))
                if j == J - 1:
                    op.then_inc(p_dve if g != 0 else p_dve_half, 1)

            def p_lo_part(b, i, g):
                dve.wait_ge(p_hi, 2 * (b * J + i) + g + 1)
                lo(pT_lo[:, JH * g:JH * (g + 1), :].rearrange("p a n -> p (a n)"), p_bank(g),
                   pT_hi[:, JH * g:JH * (g + 1), :].rearrange("p a n -> p (a n)"), p_lo)

            def shifted_rows(b, k, rows):
                n, j = b * J + k, gate_tile(b, k)
                if j == 0:
                    dve.wait_ge(ld_before, 16 * (b + 1))
                before = x_before[:] if j == 0 else tile(b, j - 1)
                row = rows[:, k % 2, :]
                tt(row, before, tile(b, j), ALU.subtract).then_inc(xr_sub, 1)
                dve.wait_ge(xr_sub, n + 1)
                tt(row, row, mr_row[:], ALU.mult).then_inc(xr_mul, 1)
                dve.wait_ge(xr_mul, n + 1)
                tt(row, row, tile(b, j), ALU.add).then_inc(xr_ok, 1)

            def batch(b, first, last=False):
                if not first:
                    x_split(b, 0)
                    pv_evacuate(b - 1, J - 1)
                x_split(b, 1)
                z_split(b, 0, 0)
                if first:
                    dve.wait_ge(earlier_done, 1)
                    link(nc.vector.tensor_copy(rank[:, :, 0, :], counts_ps.rearrange("p (b e) -> p b e", b=B)))
                    dve.wait_ge(wv_hi_ok, 1)
                    lo(wv_lo[:].rearrange("p c n -> p (c n)"), wv2_raw[:].rearrange("p c n -> p (c n)"),
                       wv_hi[:].rearrange("p c n -> p (c n)"), wv_lo_ok)
                for i in range(J):
                    dve.wait_ge(s_done, b * J + i + 1)
                    nc.vector.tensor_reduce(neg_max[:, i:i + 1], score_ps, AX.X, ALU.max, negate=True
                                            ).then_inc(max_done, 1)
                    dve.wait_ge(exp_done, b * J + i + 1)
                    if not (first and i == 0):
                        dve.wait_ge(p_act, b * J + i)
                    nc.vector.transpose(prob_t[:], prob[:]).then_inc(p_blocks, 1)
                    nc.vector.reciprocal(row_inv[:, i:i + 1], row_sum[:, i:i + 1]).then_inc(inv_ok, 1)
                    dve.wait_ge(p_blocks, b * J + i + 1)
                    for j in range(J):
                        p_move(j, None if i < J - 1 else 0)
                        if i == 0:
                            dve.wait_ge(out_hi, HI(b, DC + j) + 1)
                            lo(v_lo[:, j, :], out_bank(OUT0 + DC + j), v_hi[:, j, :], out_free)
                    if i:
                        pv_evacuate(b, i - 1)
                    for g in range(2):
                        p_lo_part(b, i, g)
                        if i == J - 1 and g == 0:
                            for j in range(J):
                                p_move(j, 1)
                    if i == 3:
                        dve.wait_ge(row_done, b + 1)
                        dve.wait_ge(ld_brow, 16 * (b + 1))
                        tt(b_row[:], row_ps, b_row[:], ALU.add).then_inc(row_ok, 1)
                    if first and i == 0:
                        token_slots()
                    if last and i in (1, 2):
                        if i == 1:
                            dve.wait_ge(x1_ok, J)
                        shifted_rows(0, i - 1, xr_early)
                    if i == JH - 1:
                        z_split(b, 15, 12)

            batch(0, True)
            with dve.Fori(1, B - 1) as b:
                batch(b, False)
            batch(B - 1, False, True)

            def unit_split(e, u):
                dve.wait_ge(w_hi, WH(e, u) + 1)
                lo(wu_lo[:, u, :], w_raw[:, u % RAW, :], wu_hi[:, u, :], w_lo)

            def row_blocks(e, first):
                dve.wait_ge(ld_xrow, 16 * (e + 1))
                if not first:
                    dve.wait_ge(r_act, e - 1)
                nc.vector.transpose(row_t[:].rearrange("p t d -> p (t d)"), xrow[:].rearrange("p t d -> p (t d)")
                                    ).then_inc(r_blocks, 1)
                dve.wait_ge(r_blocks, e)

            def row_moves():
                for c in range(3):
                    for a in range(4):
                        op = nc.vector.tensor_copy(*row_move(a, c))
                op.then_inc(r_dve, 1)

            def rows_split(e):
                for g in range(2):
                    dve.wait_ge(t_hi, MT(e, g) + 1)
                    lo(xe_lo[:, 2 * g:2 * g + 2, :].rearrange("p a n -> p (a n)"), ps[:, g, :],
                       xe_hi[:, 2 * g:2 * g + 2, :].rearrange("p a n -> p (a n)"), t_lo)

            def gate_split(n, k):
                dve.wait_ge(g_t_hi, n + 1)
                lo(xrT_lo[:, k % 2, :], gate_t_bank(k), xrT_hi[:, k % 2, :], g_t_lo)

            for g in range(DC):
                dve.wait_ge(t_hi, g + 1)
                lo(wrT_lo[:, g, :], tr_bank(TR0 + g), wrT_hi[:, g, :], t_lo)
            pv_evacuate(B - 1, J - 1)
            last_x1 = tile(B - 1, query(J - 1))
            dve.wait_ge(out_free, PV(B - 1, J - 1) + 1)
            tt(last_x1, last_x1, b_row[:], ALU.add).then_inc(x1_last, 1)
            gate_split(0, 0)
            shifted_rows(0, 2, xr_early)
            gate_split(1, 1)
            rows, own = xk[:, 1, :], tile(B - 1, query(0))
            dve.wait_ge(x1_ok, NT - 1)
            dve.wait_ge(scattered[1], 16 * (NT // 2 - 1))
            tt(rows, tile(B - 1, query(J - 1)), own, ALU.subtract).then_inc(xk_last, 1)
            dve.wait_ge(xk_last, 1)
            tt(rows, rows, mk_row[:], ALU.mult).then_inc(xk_last, 1)
            dve.wait_ge(xk_last, 2)
            tt(rows, rows, own, ALU.add).then_inc(xk_last, 1)
            for k in range(2, EARLY):
                gate_split(k, k)
                if k + 1 < EARLY:
                    dve.wait_ge(g_t_done, k)
                    shifted_rows(0, k + 1, xr_early)
            unit_split(0, 0)
            rows_split(0)
            for u in range(1, KU):
                if u not in POOL_UNITS:
                    unit_split(0, u)
            row_blocks(1, True)
            row_moves()

            def second_units(e):
                for u in range(KU, UNITS):
                    if u == KU + DVE_SQUARE // 2:
                        f = DVE_SQUARE
                        dve.wait_ge(relu_ok, FC * e + f + 1)
                        dve.wait_ge(h_lo_ok, FC * e + f - 1)
                        tt(hsq[:, f % 2, :], relu[:, f % 2, :], relu[:, f % 2, :], ALU.mult).then_inc(hsq_dve, 1)
                    unit_split(e, u)

            def expert(e, last):
                second_units(e - 1)
                rows_split(e)
                for u in range(KU):
                    unit_split(e, u)
                if not last:
                    row_blocks(e + 1, False)
                    row_moves()

            with dve.Fori(1, E - 1) as e:
                expert(e, False)
            expert(E - 1, True)
            second_units(E - 1)

            def scale_y(b, k):
                j = gate_tile(b, k)
                dve.wait_ge(gate_ok, b * J + k + 1)
                dve.wait_ge(y_here[j], 16 * (b + 1))
                tt(y_got[:, j, :], y_got[:, j, :], gate_at(b, k), ALU.mult).then_inc(scaled, 1)

            dve.wait_ge(h_lo_ok, FC * E)
            dve.wait_ge(x1_ok, NT - 1)
            for k in range(EARLY, J):
                if k >= EARLY + 2:
                    dve.wait_ge(g_t_done, k - 1)
                shifted_rows(0, k, xr)
                if k > EARLY:
                    gate_split(k - 1, k - 1)

            def gate_rows(b, k):
                dve.wait_ge(g_t_done, b * J + k - 1)
                shifted_rows(b, k, xr)
                gate_split(b * J + k - 1, (k - 1) % 2)

            def gates(b):
                for k in range(J):
                    gate_rows(b, k)
                    if not pool_scales(k):
                        scale_y(b - 1, k)

            gates(1)
            with dve.Fori(2, B - 1) as b:
                gates(b)
            todo = [(b, k) for b in (B - 2, B - 1) for k in range(J) if not pool_scales(k)]
            for k in range(J):
                gate_rows(B - 1, k)
                if todo[0] <= (B - 1, min(k - 2, J - ENDS - 1)):
                    scale_y(*todo.pop(0))
            gate_split(NT - 1, 1)
            for b, k in todo:
                if k < J - ENDS:
                    scale_y(b, k)
            before = (B - 1) * (J - len(POOL_SCALES)) + sum(not pool_scales(k) for k in range(J - ENDS))
            for i, k in enumerate(range(J - ENDS, J)):
                scale_y(B - 1, k)
                dve.wait_ge(scaled, before + i + 1)
                dve.wait_ge(stored[k % RES], 16 * ((B - 1) * (J // RES) + k // RES))
                tt(res[:, k % RES, :], y_got[:, k, :], tile(B - 1, k), ALU.add).then_inc(res_end, 1)

        @block.gpsimd
        def _(pool):
            chain = [0]

            def link(op):
                chain[0] += 1
                op.then_inc(pool_chain, 1)
                pool.wait_ge(pool_chain, chain[0])

            def settle():
                pool.sem_inc(settled, 1)

            tt = nc.gpsimd.tensor_tensor
            link(nc.gpsimd.memset(ident[:], 0.0))
            link(nc.gpsimd.affine_select(out=ident[:], in_=ident[:], compare_op=ALU.not_equal, fill=1.0, base=0,
                                         pattern=[[-1, P]], channel_multiplier=1))
            link(nc.gpsimd.memset(upper[:], 1.0))
            link(nc.gpsimd.affine_select(out=upper[:], in_=upper[:], compare_op=ALU.is_gt, fill=0.0, base=0,
                                         pattern=[[1, P]], channel_multiplier=-1))
            link(nc.gpsimd.memset(ones[:], 1.0))
            link(nc.gpsimd.memset(dx[:], 0.0))
            nc.gpsimd.memset(mean_w[:], -1.0 / S).then_inc(consts_ok, 1)
            nc.gpsimd.iota(own_i[:].rearrange("p (b j) -> p b j", b=B), [[S, B], [1, J]], base=N,
                           channel_multiplier=J).then_inc(own_ok, 1)
            pool.dma_start(shift_dram[:, 0, :], A["cond"]).then_inc(cond_rows, 16)
            pool.dma_start(y_dram[N:N + 1, :], dx[0:1, :]).then_inc(zero_row, 16)
            pool.wait_ge(zeroed, 16)
            pool.wait_ge(zero_row, 16)
            pool.wait_ge(cond_rows, 16)

            def x1_tile(b, i):
                pool.wait_ge(out_free, PV(b, i) + 1)
                pool.wait_ge(row_ok, b + 1)
                settle()
                row = tile(b, query(i))
                tt(row, row, b_row[:], ALU.add).then_inc(x1_ok, 1)
                pool.wait_ge(x1_ok, b * J + i + 1)

            def xk_tile(b, k, j, before):
                step = 3 * (b * J + k)
                settle()
                tt(dx[:], before, tile(b, j), ALU.subtract).then_inc(xk_step, 1)
                pool.wait_ge(xk_step, step + 1)
                tt(dx[:], dx[:], mk_row[:], ALU.mult).then_inc(xk_step, 1)
                pool.wait_ge(xk_step, step + 2)
                pool.wait_ge(scattered[k % 2], 16 * (b * (J // 2) + k // 2))
                settle()
                tt(xk[:, k % 2, :], dx[:], tile(b, j), ALU.add).then_inc(xk_step, 1)
                pool.wait_ge(xk_step, step + 3)
                settle()
                scatter(k, j)

            def scatter(k, j):
                pool.indirect_dma_start(
                    out=xk_dram, out_offset=bass.IndirectOffsetOnAxis(ap=idx_now[:, j:j + 1].bitcast(U32), axis=0),
                    in_=xk[:, k % 2, :], in_offset=None).then_inc(scattered[k % 2], 16)

            def batch(b, first, last):
                if first:
                    pool.wait_ge(index_ok, 1)
                for q in scattered:
                    pool.wait_ge(q, 16 * (J // 2) * b)
                settle()
                nc.gpsimd.tensor_copy(idx_now[:], scat_idx[:, bass.ds(b * J, J)]).then_inc(idx_copied, 1)
                steps = 2 * J - 1
                if not first:
                    pool.wait_ge(row_done, b)
                pool.wait_ge(out_free, OUT(b, DC) + 1)
                tt(dx[:], v_hi[:, 0, :].bitcast(F32), v_lo[:, 0, :].bitcast(F32), ALU.add).then_inc(vsum_step, 1)
                for k in range(1, steps):
                    j = (k + 1) // 2
                    if k % 2:
                        pool.wait_ge(out_free, OUT(b, DC + j) + 1)
                    pool.wait_ge(vsum_step, steps * b + k)
                    tt(dx[:], dx[:], (v_hi, v_lo)[(k + 1) % 2][:, j, :].bitcast(F32), ALU.add).then_inc(vsum_step, 1)
                pool.wait_ge(idx_copied, b + 1)
                for i in range(J):
                    j = query(i)
                    if last and i == J - 1:
                        pool.wait_ge(x1_last, 1)
                    else:
                        x1_tile(b, i)
                    if j == J - 1:
                        settle()
                        pool.dma_start(batch_of(shift_dram[:, 1:P + 1, :], b), tile(b, j)).then_inc(shift_out, 16)
                    if i:
                        if j == 0:
                            pool.wait_ge(shift_in, 16 * (b + 1))
                        xk_tile(b, i - 1, j, tile(b, j - 1) if j else x_before[:])
                    if j == J - 1:
                        pool.wait_ge(shift_out, 16 * (b + 1))
                        settle()
                        pool.dma_start(x_before[:], batch_of(shift_dram[:, 0:P, :], b)).then_inc(shift_in, 16)
                if not last:
                    xk_tile(b, J - 1, query(0), tile(b, query(J - 1)))
                else:
                    pool.wait_ge(xk_last, 3)
                    scatter(J - 1, query(0))

            batch(0, True, False)
            with pool.Fori(1, B - 1) as b:
                batch(b, False, False)
            batch(B - 1, False, True)
            for u in POOL_UNITS:
                pool.wait_ge(w_hi, WH(0, u) + 1)
                tt(wu_lo[:, u, :], w_raw[:, u % RAW, :], wu_hi[:, u, :].bitcast(F32), ALU.subtract
                   ).then_inc(w_lo_pool, 1)

            def hidden(e, first):
                for f in range(FC):
                    n = FC * e + f
                    pool.wait_ge(relu_ok, n + 1)
                    if f == DVE_SQUARE:
                        pool.wait_ge(hsq_dve, e + 1)
                    else:
                        tt(hsq[:, f % 2, :], relu[:, f % 2, :], relu[:, f % 2, :], ALU.mult).then_inc(hsq_ok, 1)
                        pool.wait_ge(hsq_ok, (FC - 1) * e + f + (1 if f < DVE_SQUARE else 0))
                    pool.wait_ge(h_hi_ok, n + 1)
                    tt(h_lo[:, f, :], hsq[:, f % 2, :], h_hi[:, f, :].bitcast(F32), ALU.subtract
                       ).then_inc(h_lo_ok, 1)

            def store_y(e):
                for t in range(CT):
                    pool.wait_ge(y_copied, CT * e + t + 1)
                    settle()
                    pool.dma_start(y_dram[bass.ds(e * CAP + t * P, P), :], y_out[:, t, :]).then_inc(y_stored[t], 16)

            hidden(0, True)
            with pool.Fori(1, E) as e:
                store_y(e - 1)
                hidden(e, False)
            store_y(E - 1)

            def indices(b):
                settle()
                nc.gpsimd.tensor_copy(idx_now[:], gath_idx[:, bass.ds(b * J, J)]).then_inc(idx_copied, 1)
                pool.wait_ge(idx_copied, B + b + 1)
                settle()

            def gather(j):
                pool.indirect_dma_start(
                    out=y_got[:, j, :], out_offset=None, in_=y_dram,
                    in_offset=bass.IndirectOffsetOnAxis(ap=idx_now[:, j:j + 1].bitcast(U32), axis=0)
                ).then_inc(y_here[j], 16)

            for q in scattered:
                pool.wait_ge(q, 16 * NT // 2)
            for q in y_stored:
                pool.wait_ge(q, 16 * E)
            indices(0)
            for k in range(J):
                gather(gate_tile(0, k))

            def batch_results(b, first, last):
                for k in range(J - ENDS if last else J):
                    n, j = b * J + k, gate_tile(b, k)
                    pool.wait_ge(y_here[j], 16 * (b + 1))
                    if pool_scales(k):
                        pool.wait_ge(gate_ok, n + 1)
                        tt(y_got[:, j, :], y_got[:, j, :], gate_at(b, k), ALU.mult).then_inc(scaled_pool, 1)
                        pool.wait_ge(scaled_pool, scaled_at(b, k))
                    else:
                        pool.wait_ge(scaled, scaled_at(b, k))
                    if not (first and k < RES):
                        pool.wait_ge(stored[k % RES], 16 * (b * (J // RES) + k // RES))
                    settle()
                    tt(res[:, k % RES, :], y_got[:, j, :], tile(b, j), ALU.add).then_inc(res_ok, 1)
                    if not last:
                        settle()
                        nc.gpsimd.tensor_copy(idx_now[:, j:j + 1], gath_idx[:, bass.ds((b + 1) * J + j, 1)]
                                              ).then_inc(idx_copied, 1)
                        pool.wait_ge(idx_copied, B + 1 + n + 1)
                        pool.wait_ge(res_ok, n + 1)
                        settle()
                        gather(j)

            batch_results(0, True, False)
            with pool.Fori(1, B - 1) as b:
                batch_results(b, False, False)
            batch_results(B - 1, False, True)

        @block.tensor
        def _(pe):
            def mm3(out, l_hi, l_lo, r_hi, r_lo, start, stop):
                nc.tensor.matmul(out, l_hi, r_hi, start=start, stop=False)
                nc.tensor.matmul(out, l_hi, r_lo, start=False, stop=False)
                return nc.tensor.matmul(out, l_lo, r_hi, start=False, stop=stop)

            pe.wait_ge(consts_ok, 1)
            for k in range(2 * DC):
                if k % 2 == 0:
                    pe.wait_ge(ld_wqk[k // 2], 16)
                raw = (wq_raw, wk_raw)[k // DC]
                for c in range(DC):
                    op = nc.tensor.transpose(tr_bank(k)[:, c * P:(c + 1) * P],
                                             raw[:, c, (k % DC) * P:(k % DC + 1) * P], ident[:])
                op.then_inc(tr_done, 1)

            def transpose_x(b, p, first):
                pe.wait_ge(ld_x, 16 * (2 * b + p + 1))
                for c in range(DC):
                    if c == 0 and p == 0 and not first:
                        pe.wait_ge(exp_done, b * J)
                        pe.wait_ge(row_ok, b)
                    pe.wait_ge(tr_lo, (1, 2, 5, 6)[c] if first and p == 0 else TR(b, DC * p + c) - 3)
                    for t in range(JH):
                        op = nc.tensor.transpose(tr_bank(TR0 + DC * p + c)[:, t * P:(t + 1) * P],
                                                 x_in[:, t, c * P:(c + 1) * P], ident[:])
                    op.then_inc(tr_done, 1)

            transpose_x(0, 0, True)
            pe.wait_ge(tr_lo, 2 * DC)
            for t in range(DC):
                if t >= 2:
                    pe.wait_ge(out_free, t - 1)
                for c in range(DC):
                    op = mm3(out_bank(t), wqT_hi[:, c, t * P:(t + 1) * P], wqT_lo[:, c, t * P:(t + 1) * P],
                             wkT_hi[:, c, :], wkT_lo[:, c, :], c == 0, c == DC - 1)
                op.then_inc(out_done, 1)
                if t == DC - 2:
                    pe.wait_ge(ld_small, 16 * 6)
                    for c in range(DC):
                        op = nc.tensor.transpose(misc_ps[:, c * B:(c + 1) * B], cond4[:, c * P:(c + 1) * P],
                                                 ident[0:B, 0:B])
                    op.then_inc(misc_done, 1)
            pe.wait_ge(misc_ok, 1)
            pe.wait_ge(out_free, 3)
            pe.wait_ge(ld_wv1, 16)
            for c in range(DC):
                op = nc.tensor.matmul(out_bank(4)[0:B, :], condT[:, c, :], wv1_raw[:, c, :],
                                      start=(c == 0), stop=(c == DC - 1))
            op.then_inc(out_done, 1)
            pe.wait_ge(tot_ok, 1)
            nc.tensor.matmul(counts_ps, upper[:], tot[:].rearrange("p b e -> p (b e)"), start=True, stop=False)
            nc.tensor.matmul(counts_ps, ones[:], earlier[:].rearrange("p b e -> p (b e)"), start=False, stop=True
                             ).then_inc(earlier_done, 1)

            def z_tiles(b, p):
                k0, h = 15 if p else 0, half(p)
                pe.wait_ge(tr_lo, TR(b, DC * (p + 1) - 1) + 1)
                for t in range(DC):
                    pe.wait_ge(out_free, OUT(b, k0 + t) - 1)
                    for c in range(DC):
                        op = mm3(out_bank(OUT0 + k0 + t), m_hi[:, c, t * P:(t + 1) * P], m_lo[:, c, t * P:(t + 1) * P],
                                 xT_hi[:, c, h * SH:(h + 1) * SH], xT_lo[:, c, h * SH:(h + 1) * SH],
                                 c == 0, c == DC - 1)
                    op.then_inc(out_done, 1)

            def v_tiles(b):
                for j in range(J):
                    pe.wait_ge(out_free, OUT(b, DC + j) - 1)
                    for c in range(DC):
                        op = mm3(out_bank(OUT0 + DC + j), xT_hi[:, c, j * P:(j + 1) * P], xT_lo[:, c, j * P:(j + 1) * P],
                                 wv_hi[:, c, :], wv_lo[:, c, :], c == 0, c == DC - 1)
                    op.then_inc(out_done, 1)

            def scores(b, i):
                q = (i % JH) * P
                if i:
                    pe.wait_ge(exp_done, b * J + i)
                for k in range(2):
                    for c in range(DC):
                        if i % JH == 0 and k == 0:
                            pe.wait_ge(out_free, OUT(b, (15 if i else 0) + c) + 1)
                        if i == 0 and k == 0 and c == 0:
                            pe.wait_ge(tr_lo, TR(b, 2 * DC - 1) + 1)
                        op = mm3(ps[:, k, :], z_hi[:, c, q:q + P], z_lo[:, c, q:q + P],
                                 xT_hi[:, c, k * SH:(k + 1) * SH], xT_lo[:, c, k * SH:(k + 1) * SH],
                                 c == 0, c == DC - 1)
                op.then_inc(s_done, 1)

            def values(b, i):
                pe.wait_ge(out_free, PV(b, i) - 1)
                for j in range(J):
                    if j % JH == 0:
                        pe.wait_ge(p_lo, 2 * (b * J + i) + j // JH + 1)
                    if i == 0 and j == 0:
                        pe.wait_ge(out_free, OUT(b, 2 * DC + JH - 1) + 1)
                    op = mm3(out_bank(PV(0, i)), pT_hi[:, j, :], pT_lo[:, j, :], v_hi[:, j, :], v_lo[:, j, :],
                             j == 0, j == J - 1)
                op.then_inc(out_done, 1)

            def mean_row(b):
                pe.wait_ge(vsum_step, (2 * J - 1) * (b + 1))
                pe.wait_ge(mean_ok, 1)
                nc.tensor.matmul(row_ps, mean_w[:], dx[:], start=True, stop=True).then_inc(row_done, 1)

            def batch(b, first):
                if not first:
                    transpose_x(b, 0, first)
                    values(b - 1, J - 1)
                transpose_x(b, 1, first)
                z_tiles(b, 0)
                scores(b, 0)
                if first:
                    pe.wait_ge(wv_lo_ok, 1)
                v_tiles(b)
                for i in range(1, J):
                    scores(b, i)
                    values(b, i - 1)
                    if i == 3:
                        mean_row(b)
                    if i == JH - 1:
                        z_tiles(b, 1)

            batch(0, True)
            with pe.Fori(1, B) as b:
                batch(b, False)
            pe.wait_ge(ld_wr, 16)
            pe.wait_ge(exp_done, B * J)
            pe.wait_ge(row_ok, B)
            for g in range(DC):
                for c in range(DC):
                    op = nc.tensor.transpose(tr_bank(TR0 + g)[:, c * P:(c + 1) * P], wr_raw[:, c, g * P:(g + 1) * P],
                                             ident[:])
                op.then_inc(t_done, 1)
            values(B - 1, J - 1)

            def transpose_xr(n, k, rows, first):
                pe.wait_ge(xr_ok, n + 1)
                if not (first and k < 2):
                    pe.wait_ge(g_t_lo, n - 1)
                for c in range(DC):
                    op = nc.tensor.transpose(gate_t_bank(k)[:, c * P:(c + 1) * P],
                                             rows[:, k % 2, c * P:(c + 1) * P], ident[:])
                op.then_inc(g_t_done, 1)

            def gate_product(n, k, first):
                pe.wait_ge(g_t_lo, n + 1)
                if not (first and k < 2):
                    pe.wait_ge(gate_ok, n - 1)
                if first and k == 1:
                    pe.wait_ge(out_free, PV(B - 1, J - 1) + 1)
                for c in range(DC):
                    if first and k == 0:
                        pe.wait_ge(t_lo, c + 1)
                    op = mm3(gate_bank(k), xrT_hi[:, k % 2, c * P:(c + 1) * P], xrT_lo[:, k % 2, c * P:(c + 1) * P],
                             wrT_hi[:, c, :], wrT_lo[:, c, :], c == 0, c == DC - 1)
                op.then_inc(g_done, 1)

            transpose_xr(0, 0, xr_early, True)
            for k in range(EARLY):
                if k + 1 < EARLY:
                    transpose_xr(k + 1, k + 1, xr_early, True)
                gate_product(k, k, True)

            def transpose_rows(e):
                pe.wait_ge(ld_xrow, 16 * (e + 1))
                pe.wait_ge(t_lo, DC)
                for g in range(2):
                    for c in range(2):
                        for t in range(CT):
                            op = nc.tensor.transpose(ps[:, g, c * CAP + t * P:c * CAP + (t + 1) * P],
                                                     xrow[:, t, (2 * g + c) * P:(2 * g + c + 1) * P], ident[:])
                    op.then_inc(t_done, 1)

            def hidden(e, first):
                for f in range(FC):
                    u = f // 2
                    if f % 2 == 0:
                        wait_lo(pe, e, u)
                    if not (first and f < 4):
                        pe.wait_ge(relu_ok, FC * e + f - 3)
                    for c in range(DC):
                        if f == 0 and c % 2 == 0:
                            pe.wait_ge(t_lo, MT(e, c // 2) + 1)
                        at = c * CAP + (f % 2) * P
                        op = mm3(ps[:, 2 + f % 4, 0:CAP], wu_hi[:, u, at:at + P], wu_lo[:, u, at:at + P],
                                 xe_hi[:, c, :], xe_lo[:, c, :], c == 0, c == DC - 1)
                    op.then_inc(h_done, 1)

            def expert_out_half(e, t):
                for f in range(FC):
                    u = KU + f // 2
                    if t == 0:
                        pe.wait_ge(h_lo_ok, FC * e + f + 1)
                        if f % 2 == 0:
                            wait_lo(pe, e, u)
                    at = (f % 2) * D
                    op = mm3(ps[:, 6 + t, :], h_hi[:, f, t * P:(t + 1) * P], h_lo[:, f, t * P:(t + 1) * P],
                             wu_hi[:, u, at:at + D], wu_lo[:, u, at:at + D], f == 0, f == FC - 1)
                    if t == CT - 1 and f % 2 and f < FC - 1:
                        op.then_inc(v_used, 1)
                op.then_inc(y_done, 1)

            def expert_out(e):
                for t in range(CT):
                    expert_out_half(e, t)

            transpose_rows(0)
            hidden(0, True)
            pe.wait_ge(gate_ok, EARLY)
            with pe.Fori(1, E) as e:
                expert_out(e - 1)
                hidden(e, False)
                pe.wait_ge(y_copied, CT * e)

            expert_out_half(E - 1, 0)
            transpose_xr(EARLY, EARLY, xr, True)
            expert_out_half(E - 1, 1)
            for n in range(EARLY + 1, J):
                transpose_xr(n, n, xr, True)
                if n == EARLY + 1:
                    pe.wait_ge(y_copied, CT * E)
                gate_product(n - 1, n - 1, True)
            with pe.Fori(2, NT // 4) as q:
                for k in range(4):
                    transpose_xr(4 * q + k, k, xr, False)
                    gate_product(4 * q + k - 1, (k - 1) % 4, False)
            gate_product(NT - 1, 3, False)


_INS = {"x": "x", "cond": "cond_1024", "tok": "itok_BxS_2_50255", "Wq2": "L0_cond_Wq2", "bq2": "L0_cond_bq2",
        "Wk2": "L0_cond_Wk2", "Wv": "L0_cond_Wv", "bv": "L0_cond_bv", "alpha": "L0_cond_alpha",
        "mk": "L1_cond_time_maa_k", "mr": "L1_cond_time_maa_r", "w_recept": "L1_cond_w_recept",
        "w_key": "L1_cond_w_key", "w_value": "L1_cond_w_value"}


def kernel(**inputs):
    import numpy as _np
    import concourse.bacc as _bacc
    from concourse import mybir as _mybir
    from concourse.bass_utils import run_bass_kernel_spmd as _run

    nc = _bacc.Bacc("TRN2", target_bir_lowering=False, num_devices=1, dynamic_dma_scratch_size=4096)
    arrays, args = {}, {}
    for short, name in _INS.items():
        a = _np.ascontiguousarray(inputs[name])
        arrays[f"in_{name}"] = a
        args[short] = nc.dram_tensor(f"in_{name}", a.shape, _mybir.dt.from_np(a.dtype), kind="ExternalInput").ap()
    args["out"] = nc.dram_tensor("out_0", inputs["x"].shape, _mybir.dt.float32, kind="ExternalOutput").ap()
    build(nc, args)
    r = _run(nc, [arrays], core_ids=[0])
    return r.results[0]["out_0"]
```
